# Optimizing a Trainium2 kernel written in Bass

```python
import numpy as np
import jax
import jax.numpy as jnp

def _softmax(x, axis=-1):
    return jax.nn.softmax(x, axis=axis)

def _gelu(x):
    return jax.nn.gelu(x, approximate=True)

def _silu(x):
    return jax.nn.silu(x)

def _sigmoid(x):
    return jax.nn.sigmoid(x)

def _layernorm(x, axis=-1, eps=1e-05):
    m = jnp.mean(x, axis=axis, keepdims=True)
    v = jnp.var(x, axis=axis, keepdims=True)
    return (x - m) / jnp.sqrt(v + eps)

def _scatter_add(tgt, idx, src, axis=0):
    return tgt.at[idx].add(src)

def _segment_sum(src, seg, n):
    return jax.ops.segment_sum(src, seg, n)
kernel_name = 'mk_adj_resnorm_d1_adj_r2_415db8'

def setup_inputs(seed: int=0):
    np.random.seed(seed)
    _w = jnp.asarray

    def _rec_inputs():
        import jax
        import jax.numpy as jnp
        _gk = jax.random.key(seed)
        x = -0.001547 + 1.001 * jax.random.normal(jax.random.fold_in(_gk, 1), (512, 128), jnp.float32)
        _a = jax.random.bernoulli(jax.random.fold_in(_gk, 2), 0.03125, (512, 512))
        adj = _a.astype(jnp.int32)
        return (x, adj)
    x, adj = _rec_inputs()

    def _L0_gnn_setup():
        import jax, jax.numpy as jnp
        import numpy as np
        BT, BN, D, H = (512, 512, 128, 8)
        DH = D // H
        key = jax.random.key(seed)
        ks = jax.random.split(key, 16)
        s = 1.0 / np.sqrt(D)
        return {'h_target': jax.random.normal(ks[0], (BT, D), jnp.float32), 'h_neigh': jax.random.normal(ks[1], (BN, D), jnp.float32), 'adjacency': jax.random.randint(ks[2], (BT, BN), 0, 2, jnp.int32), 'edge_types': jax.random.randint(ks[3], (BT, BN), 0, 2, jnp.int32), 'Wq': jax.random.normal(ks[4], (D, D), jnp.float32) * s, 'bq': jnp.zeros((D,), jnp.float32), 'Wk': jax.random.normal(ks[5], (D, D), jnp.float32) * s, 'bk': jnp.zeros((D,), jnp.float32), 'Wv': jax.random.normal(ks[6], (D, D), jnp.float32) * s, 'bv': jnp.zeros((D,), jnp.float32), 'Wo': jax.random.normal(ks[7], (D, D), jnp.float32) * s, 'bo': jnp.zeros((D,), jnp.float32), 'E': jax.random.normal(ks[8], (2, D), jnp.float32)}
    _L0_gnn_all = _L0_gnn_setup()
    _L0_gnn_in = {k: v for k, v in _L0_gnn_all.items() if k in ('h_neigh', 'Wq', 'bq', 'Wk', 'bk', 'Wv', 'bv', 'Wo', 'bo', 'E')}
    del _L0_gnn_all
    return {'x': x, 'adj': adj, 'L0_gnn_h_neigh': _L0_gnn_in['h_neigh'], 'L0_gnn_Wq': _L0_gnn_in['Wq'], 'L0_gnn_bq': _L0_gnn_in['bq'], 'L0_gnn_Wk': _L0_gnn_in['Wk'], 'L0_gnn_bk': _L0_gnn_in['bk'], 'L0_gnn_Wv': _L0_gnn_in['Wv'], 'L0_gnn_bv': _L0_gnn_in['bv'], 'L0_gnn_Wo': _L0_gnn_in['Wo'], 'L0_gnn_bo': _L0_gnn_in['bo'], 'L0_gnn_E': _L0_gnn_in['E']}

def reference(x, adj, L0_gnn_h_neigh, L0_gnn_Wq, L0_gnn_bq, L0_gnn_Wk, L0_gnn_bk, L0_gnn_Wv, L0_gnn_bv, L0_gnn_Wo, L0_gnn_bo, L0_gnn_E):
    import jax
    import jax.numpy as jnp

    def _L0_gnn_ref(h_target, h_neigh, adjacency, edge_types, Wq, bq, Wk, bk, Wv, bv, Wo, bo, E):
        import jax, jax.numpy as jnp
        import numpy as np
        BT, BN, D, H = (512, 512, 128, 8)
        DH = D // H
        Bt, d = h_target.shape
        Bn = h_neigh.shape[0]
        msg = h_neigh[None, :, :] + E[edge_types]
        q = (h_target @ Wq.T + bq).reshape(Bt, H, DH)
        k = (msg @ Wk.T + bk).reshape(Bt, Bn, H, DH)
        v = (msg @ Wv.T + bv).reshape(Bt, Bn, H, DH)
        scores = jnp.einsum('bhd,bnhd->bhn', q, k) / np.sqrt(DH).astype(np.float32)
        mask = adjacency[:, None, :] == 0
        scores = jnp.where(mask, jnp.float32(-1000000000.0), scores)
        attn = jax.nn.softmax(scores, axis=-1)
        attn = jnp.where(mask, jnp.float32(0.0), attn)
        out = jnp.einsum('bhn,bnhd->bhd', attn, v).reshape(Bt, d)
        return out @ Wo.T + bo
    x = _layernorm(x + _L0_gnn_ref(x, L0_gnn_h_neigh, adj, adj, L0_gnn_Wq, L0_gnn_bq, L0_gnn_Wk, L0_gnn_bk, L0_gnn_Wv, L0_gnn_bv, L0_gnn_Wo, L0_gnn_bo, L0_gnn_E), axis=-1)
    return x

_drawn_inputs = setup_inputs


def setup_inputs(seed=0):
    import zlib

    import numpy as np

    out = dict(_drawn_inputs(seed))
    spreads = {'L0_gnn_bq': (0.0, 0.454),
     'L0_gnn_bk': (0.0, 0.8),
     'L0_gnn_bv': (0.0, 0.1),
     'L0_gnn_bo': (0.0, 0.1)}
    factors = {}
    for name, (base, spread) in spreads.items():
        noise = np.random.default_rng([zlib.crc32(name.encode()), seed]).standard_normal(out[name].shape)
        drawn = base * np.exp(spread * noise) if base else spread * noise
        out[name] = jnp.asarray(drawn.astype(out[name].dtype))
    for name, factor in factors.items():
        out[name] = (out[name] * factor).astype(out[name].dtype)
    return out
```

```python
from contextlib import ExitStack

import numpy as np

import concourse.bass as bass
from concourse import mybir

F32 = mybir.dt.float32
BF16 = mybir.dt.bfloat16
I32 = mybir.dt.int32
ALU = mybir.AluOpType
AX = mybir.AxisListType
ACT = mybir.ActivationFunctionType

P = 128
BT = BN = 512
D = 128
H = 8
DH = D // H
NT = BN // P
QUAD = 4
HALF = BT // 2
TPC = HALF // P
COL = P // QUAD
GROUPS = [(1, 1), (1, 2), (2, 1), (2, 2), (1, 3), (3, 1)]
MAXROWS = 3 * DH
SPLIT = len(GROUPS) * DH
KROWS = SPLIT + 2
SCALE = 1.0 / DH ** 0.5
BIG = float(2.0 ** 100)
FLOOR = -float(2.0 ** 99)
LEAST = -float(2.0 ** 98)
TINY = 1e-30
EPS = 1e-5

CHUNKS = [(half, quad) for half in range(BT // HALF) for quad in range(H // QUAD)]
STEPS = [(c, t) for c in range(len(CHUNKS)) for t in range(NT)]
UNITS = [(c, i, g) for c in range(len(CHUNKS)) for i in range(TPC) for g in range(QUAD)]
PER_CHUNK = TPC * QUAD
AHEAD = 12
PV_LAG = 2


def units_in(s):
    return range(min(AHEAD + 2 * s, len(UNITS)), min(AHEAD + 2 * s + 2, len(UNITS)))


SHIFT_AT = {4 * c - 2: c for c in range(1, len(CHUNKS))}
SUMMED_AT = {4 * c + 3 + PV_LAG: c for c in range(len(CHUNKS))}
SUMS_AT = {4 * c + 7: c for c in range(len(CHUNKS))}
OUT_AT = {13: 0, 20: 1}
LAST = 20
MISC_ORDER = [("shift", 0), ("shift", 1), ("shift", 2), ("sums", 0), ("shift", 3), ("sums", 1),
              ("out", 0), ("sums", 2), ("sums", 3), ("out", 1)]


def attention_kernel(nc, kin, qin, vin, x, bv, bo, adj, adj_t, out):
    with ExitStack() as ctx:
        def sb(name, shape, dt=F32):
            return ctx.enter_context(nc.sbuf_tensor(name, shape, dt))

        def psum(name, shape, dt=F32):
            return ctx.enter_context(nc.psum_tensor(name, shape, dt))

        def sem(name):
            return ctx.enter_context(nc.semaphore(name))

        ps_max = [psum(f"ps_max{i}", [P, BN]) for i in range(2)]
        ps_s = [psum(f"ps_s{i}", [P, QUAD, HALF]) for i in range(2)]
        ps_o = psum("ps_o", [P, 2, HALF])
        misc = psum("misc", [P, 512])
        misc_bf = misc[:].bitcast(BF16).rearrange("p (h b) -> p h b", h=QUAD)
        ps_k, ps_q, ps_v = ps_s[0][:, 0:2, :], ps_s[1][:, 0:2, :], ps_s[0][:, 2:4, :]

        kin_sb = sb("kin_sb", [P, BN + D + 3])
        qin_sb = sb("qin_sb", [P, BT + D + 1])
        vin_sb = sb("vin_sb", [P, D + 2 * D])
        x_sb = sb("x_sb", [P, BT // P, D])
        bv_sb = sb("bv_sb", [P, D])
        bo_sb = sb("bo_sb", [P, D])
        adj_sb = sb("adj_sb", [P, BT // P, BN], I32)
        adj_t_sb = sb("adj_t_sb", [P, NT, BT], I32)
        mask_max = sb("mask_max", [P, BT // P, BN], BF16)
        no_edge = sb("no_edge", [P, NT, BT], BF16)
        msg = sb("msg", [P, BN])
        k_part = [sb(f"k{i}", [P, BN], BF16) for i in (1, 2, 3)]
        q_part = [sb(f"q{i}", [P, BT], BF16) for i in (1, 2, 3)]
        k_rest = sb("k_rest", [P, BN])
        q_rest = sb("q_rest", [P, BT])
        k_stack = sb("k_stack", [P, H, BN], BF16)
        q_stack = sb("q_stack", [P, H, BT], BF16)
        v_ones = sb("v_ones", [P, NT, H, COL])
        ident = sb("ident", [P, P], BF16)
        minus_big = sb("minus_big", [P, P], BF16)
        pick = sb("pick", [P, P])
        tiny = sb("tiny", [P, 1])
        tiny4 = sb("tiny4", [P, QUAD])
        masked = sb("masked", [P, 2, BN], BF16)
        peak = sb("peak", [P, len(UNITS)])
        shift = sb("shift", [P, len(UNITS)])
        shift_part = sb("shift_part", [P, len(UNITS), 2], BF16)
        probs = sb("probs", [P, len(STEPS), QUAD, HALF])
        o_sb = sb("o_sb", [P, len(CHUNKS), HALF])
        r_sum = sb("r_sum", [P, len(CHUNKS), HALF])
        o_norm = sb("o_norm", [P, len(CHUNKS), HALF])
        xb = sb("xb", [P, BT // P, D])
        res = sb("res", [P, BT // P, D])
        stats = sb("stats", [P, BT // P, 6])
        mean_var = sb("mean_var", [P, BT // P, 2])
        veps = sb("veps", [P, BT // P, 1])
        std = sb("std", [P, BT // P, 1])
        rstd = sb("rstd", [P, BT // P, 1])
        y_sb = sb("y_sb", [P, BT // P, D])

        kin_in, qin_in, vin_in = sem("kin_in"), sem("qin_in"), sem("vin_in")
        x_in, bv_in, bo_in = sem("x_in"), sem("bv_in"), sem("bo_in")
        adj_in, adj_t_in = sem("adj_in"), sem("adj_t_in")
        k_grp = [sem(f"k_grp{i}") for i in range(6)]
        q_grp = [sem(f"q_grp{i}") for i in range(6)]
        consts_ready, zeroed = sem("consts_ready"), sem("zeroed")
        ones_ready, minus_ready = sem("ones_ready"), sem("minus_ready")
        tiny_ready = sem("tiny_ready")
        msg_ready, xb_ready = sem("msg_ready"), sem("xb_ready")
        k_proj, q_proj, v_proj = sem("k_proj"), sem("q_proj"), sem("v_proj")
        k1_ready, q1_ready = sem("k1_ready"), sem("q1_ready")
        k_rest_ready, q_rest_ready = sem("k_rest_ready"), sem("q_rest_ready")
        k2_ready, q2_ready = sem("k2_ready"), sem("q2_ready")
        k3_ready, q3_ready = sem("k3_ready"), sem("q3_ready")
        v_ready = sem("v_ready")
        mask_max_ready, no_edge_ready = sem("mask_max_ready"), sem("no_edge_ready")
        unit_scored, unit_maxed = sem("unit_scored"), sem("unit_maxed")
        shift_guarded, shift_part1, shift_ready = sem("shift_guarded"), sem("shift_part1"), sem("shift_ready")
        shift_turned, shift_in_stack = sem("shift_turned"), sem("shift_in_stack")
        step_scored, probs_ready = sem("step_scored"), sem("probs_ready")
        chunk_summed, o_copied = sem("chunk_summed"), sem("o_copied")
        sums_spread, sums_inverted, o_ready = sem("sums_spread"), sem("sums_inverted"), sem("o_ready")
        projected, res_ready = sem("projected"), sem("res_ready")
        stats_ready, aggregated, var_ready = sem("stats_ready"), sem("aggregated"), sem("var_ready")
        std_ready, rstd_ready = sem("std_ready"), sem("rstd_ready")
        y_ready, y_out = sem("y_ready"), sem("y_out")

        misc_reader = {"shift": shift_in_stack, "sums": sums_inverted, "out": res_ready}

        def misc_free(eng, stage, n):
            at = MISC_ORDER.index((stage, n))
            if at:
                before, m = MISC_ORDER[at - 1]
                eng.wait_ge(misc_reader[before], m + 1)

        w_k, b_k, e_1 = kin_sb[:, BN:BN + D], kin_sb[:, BN + D:BN + D + 1], kin_sb[:, BN + D + 2:BN + D + 3]
        w_q, b_q = qin_sb[:, BT:BT + D], qin_sb[:, BT + D:BT + D + 1]
        w_v = vin_sb[:, 0:D]

        def stack_group(eng, stack, part, group, done):
            eng.dma_start(stack[group * DH:(group + 1) * DH, :, :], part[:]).then_inc(done, 16)

        block = ctx.enter_context(nc.Block())

        @block.sync
        def _(sp):
            sp.dma_start(kin_sb[:], kin).then_inc(kin_in, 16)
            sp.dma_start(adj_sb[:], adj.rearrange("(t p) n -> p t n", p=P)).then_inc(adj_in, 16)
            sp.dma_start(adj_t_sb[:], adj_t.rearrange("(t p) b -> p t b", p=P)).then_inc(adj_t_in, 16)
            sp.wait_ge(k1_ready, 1)
            for i in (0, 2, 5):
                stack_group(sp, k_stack, k_part[0], i, k_grp[i])
            sp.wait_ge(k2_ready, 1)
            for i in (1, 3):
                stack_group(sp, k_stack, k_part[1], i, k_grp[i])
            sp.wait_ge(k3_ready, 1)
            stack_group(sp, k_stack, k_part[2], 4, k_grp[4])
            out_v = out.rearrange("(t p) d -> p t d", p=P)
            for half in range(2):
                sp.wait_ge(y_ready, TPC * (half + 1))
                ts = slice(TPC * half, TPC * (half + 1))
                sp.dma_start(out_v[:, ts, :], y_sb[:, ts, :]).then_inc(y_out, 16)
            sp.wait_ge(y_out, 32)

        @block.gpsimd
        def _(pool):
            pool.dma_start(vin_sb[:], vin).then_inc(vin_in, 16)
            pool.dma_start(x_sb[:], x.rearrange("(t p) d -> p t d", p=P)).then_inc(x_in, 16)
            pool.dma_start(bv_sb[:], bv.partition_broadcast(P)).then_inc(bv_in, 16)
            pool.dma_start(bo_sb[:], bo.partition_broadcast(P)).then_inc(bo_in, 16)
            nc.gpsimd.memset(ident[:], 0.0).then_inc(zeroed, 1)
            nc.gpsimd.memset(minus_big[:], 0.0).then_inc(zeroed, 1)
            nc.gpsimd.memset(pick[:], 0.0).then_inc(zeroed, 1)
            nc.gpsimd.memset(tiny4[:], 0.0).then_inc(zeroed, 1)
            pool.wait_ge(zeroed, 4)
            for tile, fill in ((ident, 1.0), (minus_big, -BIG)):
                nc.gpsimd.affine_select(out=tile[:], in_=tile[:], compare_op=ALU.not_equal, fill=fill,
                                        base=0, pattern=[[-1, P]], channel_multiplier=1).then_inc(consts_ready, 1)
            grid = pick[:].rearrange("p (g j) -> p g j", g=QUAD)
            nc.gpsimd.affine_select(out=grid, in_=grid, compare_op=ALU.not_equal, fill=1.0, base=-DH,
                                    pattern=[[-COL, QUAD], [0, COL]],
                                    channel_multiplier=1).then_inc(consts_ready, 1)
            nc.gpsimd.affine_select(out=tiny4[:], in_=tiny4[:], compare_op=ALU.not_equal, fill=TINY, base=-DH,
                                    pattern=[[-COL, QUAD]], channel_multiplier=1).then_inc(consts_ready, 1)
            nc.gpsimd.memset(v_ones[:, :, :, DH:COL], 1.0).then_inc(ones_ready, 1)
            pool.wait_ge(ones_ready, 1)
            nc.gpsimd.memset(k_stack[SPLIT:KROWS, :, :], -1.0).then_inc(minus_ready, 1)
            pool.wait_ge(minus_ready, 1)
            pool.wait_ge(adj_t_in, 16)
            for t in range(NT):
                nc.gpsimd.tensor_scalar(no_edge[:, t, :], adj_t_sb[:, t, :], 0.0, None,
                                        ALU.is_equal).then_inc(no_edge_ready, 1)
            pool.wait_ge(x_in, 16)
            pool.wait_ge(bo_in, 16)
            for t in range(BT // P):
                nc.gpsimd.tensor_tensor(xb[:, t, :], x_sb[:, t, :], bo_sb[:], ALU.add).then_inc(xb_ready, 1)

        @block.scalar
        def _(act):
            act.dma_start(qin_sb[:], qin).then_inc(qin_in, 16)
            act.wait_ge(kin_in, 16)
            act.wait_ge(k_proj, 1)
            nc.scalar.activation(k_part[0][:], ps_k, ACT.Identity, bias=b_k).then_inc(k1_ready, 1)
            act.wait_ge(qin_in, 16)
            act.wait_ge(q_proj, 1)
            nc.scalar.activation(q_part[0][:], ps_q, ACT.Identity, bias=b_q).then_inc(q1_ready, 1)
            act.wait_ge(q1_ready, 1)
            for i in (0, 1, 4):
                stack_group(act, q_stack, q_part[0], i, q_grp[i])
            act.wait_ge(q2_ready, 1)
            for i in (2, 3):
                stack_group(act, q_stack, q_part[1], i, q_grp[i])
            act.wait_ge(q3_ready, 1)
            stack_group(act, q_stack, q_part[2], 5, q_grp[5])

            def shift_rows(c):
                half, quad = CHUNKS[c]
                act.wait_ge(shift_turned, c + 1)
                nc.scalar.activation(
                    q_stack[SPLIT:KROWS, QUAD * quad:QUAD * (quad + 1), HALF * half:HALF * (half + 1)],
                    misc_bf[SPLIT:KROWS, :, :], ACT.Copy).then_inc(shift_in_stack, 1)

            def copy_o(c):
                act.wait_ge(tiny_ready, 1)
                act.wait_ge(chunk_summed, c + 1)
                nc.scalar.activation(o_sb[:, c, :], ps_o[:, 0, :], ACT.Identity,
                                     bias=tiny[:]).then_inc(o_copied, 1)

            shift_rows(0)
            for s in range(LAST + 1):
                if s < len(STEPS):
                    act.wait_ge(step_scored, s + 1)
                    nc.scalar.activation(probs[:, s, :, :], ps_s[s % 2][:], ACT.Exp,
                                         scale=SCALE).then_inc(probs_ready, 1)
                if s in SHIFT_AT:
                    shift_rows(SHIFT_AT[s])
                if s in SUMMED_AT:
                    copy_o(SUMMED_AT[s])
            for half in range(2):
                act.wait_ge(var_ready, half + 1)
                ts = slice(TPC * half, TPC * (half + 1))
                nc.scalar.activation(std[:, ts, :], veps[:, ts, :], ACT.Sqrt).then_inc(std_ready, 1)

        @block.vector
        def _(dve):
            dve.wait_ge(kin_in, 16)
            nc.vector.tensor_scalar(msg[:], kin_sb[:, 0:BN], e_1, None, ALU.add).then_inc(msg_ready, 1)
            dve.wait_ge(consts_ready, 4)
            nc.vector.tensor_reduce(tiny[:], tiny4[:], AX.X, ALU.add).then_inc(tiny_ready, 1)

            def mask_for_max(half):
                ts = slice(TPC * half, TPC * (half + 1))
                nc.vector.tensor_scalar(mask_max[:, ts, :], adj_sb[:, ts, :], 0.0, -BIG,
                                        ALU.is_equal, ALU.mult).then_inc(mask_max_ready, 1)

            def rest(proj, bias, part, out_, first, done):
                dve.wait_ge(first, 1)
                nc.vector.scalar_tensor_tensor(out=out_[:].rearrange("p (a b) -> p a b", a=2), in0=proj,
                                               scalar=bias, in1=part[0][:].rearrange("p (a b) -> p a b", a=2),
                                               op0=ALU.add, op1=ALU.subtract).then_inc(done, 1)

            rest(ps_k, b_k, k_part, k_rest, k1_ready, k_rest_ready)
            dve.wait_ge(k_rest_ready, 1)
            nc.vector.tensor_copy(k_part[1][:], k_rest[:]).then_inc(k2_ready, 1)
            rest(ps_q, b_q, q_part, q_rest, q1_ready, q_rest_ready)
            dve.wait_ge(q_rest_ready, 1)
            nc.vector.tensor_copy(q_part[1][:], q_rest[:]).then_inc(q2_ready, 1)
            dve.wait_ge(k2_ready, 1)
            nc.vector.tensor_tensor(k_part[2][:], k_rest[:], k_part[1][:], ALU.subtract).then_inc(k3_ready, 1)
            dve.wait_ge(q2_ready, 1)
            nc.vector.tensor_tensor(q_part[2][:], q_rest[:], q_part[1][:], ALU.subtract).then_inc(q3_ready, 1)
            dve.wait_ge(adj_in, 16)
            mask_for_max(0)
            dve.wait_ge(v_proj, 1)
            dve.wait_ge(bv_in, 16)
            nc.vector.tensor_tensor(v_ones[:, :, :, 0:DH],
                                    ps_v.rearrange("p a (t h d) -> p (a t) h d", t=2, h=H),
                                    bv_sb[:].rearrange("p (o h d) -> p o h d", o=1, h=H)
                                            .broadcast_to([P, NT, H, DH]),
                                    ALU.add).then_inc(v_ready, 1)
            mask_for_max(1)

            def unit_max(u):
                c, i, g = UNITS[u]
                half, _ = CHUNKS[c]
                dve.wait_ge(mask_max_ready, half + 1)
                dve.wait_ge(unit_scored, u + 1)
                if u >= 2:
                    dve.wait_ge(unit_maxed, u - 1)
                nc.vector.tensor_tensor_reduce(masked[:, u % 2, :], ps_max[u % 2][:],
                                               mask_max[:, TPC * half + i, :], 1.0, FLOOR,
                                               ALU.add, ALU.max, peak[:, u:u + 1]).then_inc(unit_maxed, 1)
                if u % PER_CHUNK == PER_CHUNK - 1:
                    shift_parts(c)

            def shift_parts(c):
                us = slice(PER_CHUNK * c, PER_CHUNK * (c + 1))
                dve.wait_ge(unit_maxed, PER_CHUNK * (c + 1))
                nc.vector.scalar_tensor_tensor(out=shift[:, us], in0=peak[:, us], scalar=LEAST, in1=peak[:, us],
                                               op0=ALU.is_gt, op1=ALU.mult).then_inc(shift_guarded, 1)
                dve.wait_ge(shift_guarded, c + 1)
                nc.vector.tensor_copy(shift_part[:, us, 0], shift[:, us]).then_inc(shift_part1, 1)
                dve.wait_ge(shift_part1, c + 1)
                nc.vector.tensor_tensor(shift_part[:, us, 1], shift[:, us], shift_part[:, us, 0],
                                        ALU.subtract).then_inc(shift_ready, 1)

            def invert_sums(c):
                dve.wait_ge(sums_spread, c + 1)
                nc.vector.reciprocal(r_sum[:, c, :], misc[:, 0:HALF]).then_inc(sums_inverted, 1)
                dve.wait_ge(sums_inverted, c + 1)
                dve.wait_ge(o_copied, c + 1)
                nc.vector.tensor_tensor(o_norm[:, c, :], o_sb[:, c, :], r_sum[:, c, :],
                                        ALU.mult).then_inc(o_ready, 1)

            def residual(half):
                ts = slice(TPC * half, TPC * (half + 1))
                dve.wait_ge(projected, half + 1)
                dve.wait_ge(xb_ready, BT // P)
                nc.vector.tensor_tensor(res[:, ts, :], misc[:, 0:HALF].rearrange("p (t d) -> p t d", d=D),
                                        xb[:, ts, :], ALU.add).then_inc(res_ready, 1)
                dve.wait_ge(res_ready, half + 1)
                for t in range(TPC * half, TPC * (half + 1)):
                    nc.vector.bn_stats(stats[:, t, :], res[:, t, :]).then_inc(stats_ready, 1)
                for t in range(TPC * half, TPC * (half + 1)):
                    dve.wait_ge(stats_ready, t + 1)
                    nc.vector.bn_aggr(mean_var[:, t, :], stats[:, t, :]).then_inc(aggregated, 1)
                dve.wait_ge(aggregated, TPC * (half + 1))
                nc.vector.tensor_scalar(veps[:, ts, :], mean_var[:, ts, 1:2], EPS, None,
                                        ALU.add).then_inc(var_ready, 1)

            for u in range(AHEAD):
                unit_max(u)
            for s in range(LAST + 1):
                for u in units_in(s):
                    unit_max(u)
                if s in SUMS_AT:
                    invert_sums(SUMS_AT[s])
                if s in OUT_AT:
                    residual(OUT_AT[s])
            for half in range(2):
                ts = slice(TPC * half, TPC * (half + 1))
                dve.wait_ge(std_ready, half + 1)
                nc.vector.reciprocal(rstd[:, ts, :], std[:, ts, :]).then_inc(rstd_ready, 1)
                dve.wait_ge(rstd_ready, half + 1)
                for t in range(TPC * half, TPC * (half + 1)):
                    nc.vector.tensor_scalar(y_sb[:, t, :], res[:, t, :], mean_var[:, t, 0:1], rstd[:, t, :],
                                            ALU.subtract, ALU.mult).then_inc(y_ready, 1)

        @block.tensor
        def _(pe):
            pe.wait_ge(msg_ready, 1)
            nc.tensor.matmul(ps_k, w_k, msg[:], start=True, stop=True).then_inc(k_proj, 1)
            pe.wait_ge(qin_in, 16)
            nc.tensor.matmul(ps_q, w_q, qin_sb[:, 0:BT], start=True, stop=True).then_inc(q_proj, 1)
            pe.wait_ge(vin_in, 16)
            v_out = ps_v.rearrange("p a (t d) -> p (a t) d", t=2)
            for t in range(NT):
                last = nc.tensor.matmul(v_out[:, t, :], msg[:, t * P:(t + 1) * P], w_v, start=True, stop=True)
            last.then_inc(v_proj, 1)

            def unit_scores(u):
                c, i, g = UNITS[u]
                half, quad = CHUNKS[c]
                h, b = QUAD * quad + g, HALF * half + P * i
                if u >= 2:
                    pe.wait_ge(unit_maxed, u - 1)
                nc.tensor.matmul(ps_max[u % 2][:], q_stack[0:MAXROWS, h, b:b + P], k_stack[0:MAXROWS, h, :],
                                 start=True, stop=True).then_inc(unit_scored, 1)

            def turn_shift(c):
                pe.wait_ge(shift_ready, c + 1)
                misc_free(pe, "shift", c)
                for i in range(TPC):
                    for g in range(QUAD):
                        u = PER_CHUNK * c + QUAD * i + g
                        last = nc.tensor.transpose(misc_bf[SPLIT:KROWS, g, P * i:P * (i + 1)],
                                                   shift_part[:, u, :], ident[:])
                last.then_inc(shift_turned, 1)

            def step_scores(s):
                c, t = STEPS[s]
                half, quad = CHUNKS[c]
                bs = slice(HALF * half, HALF * (half + 1))
                pe.wait_ge(shift_in_stack, c + 1)
                if s >= 2:
                    pe.wait_ge(probs_ready, s - 1)
                no = no_edge[:, t, bs].rearrange("p (o b) -> p o b", o=1).broadcast_to([P, 2, HALF])
                pe.wait_ge(no_edge_ready, t + 1)
                for pair in range(QUAD // 2):
                    nc.tensor.matmul(ps_s[s % 2][:, 2 * pair:2 * pair + 2, :], minus_big[:], no,
                                     start=True, stop=False, skip_group_check=True)
                    for g in (2 * pair, 2 * pair + 1):
                        h = QUAD * quad + g
                        last = nc.tensor.matmul(ps_s[s % 2][:, g, :], k_stack[0:KROWS, h, t * P:(t + 1) * P],
                                                q_stack[0:KROWS, h, bs], start=False, stop=True,
                                                skip_group_check=True)
                last.then_inc(step_scored, 1)

            def step_values(s):
                c, t = STEPS[s]
                half, quad = CHUNKS[c]
                if t == 0 and c >= 1:
                    pe.wait_ge(o_copied, c)
                pe.wait_ge(probs_ready, s + 1)
                for g in range(QUAD):
                    last = nc.tensor.matmul(ps_o[COL * g:COL * (g + 1), 0, :], v_ones[:, t, QUAD * quad + g, :],
                                            probs[:, s, g, :], start=(t == 0), stop=(t == NT - 1))
                if t == NT - 1:
                    last.then_inc(chunk_summed, 1)

            def spread_sums(c):
                misc_free(pe, "sums", c)
                pe.wait_ge(o_copied, c + 1)
                nc.tensor.matmul(misc[:, 0:HALF], pick[:], o_sb[:, c, :], start=True,
                                 stop=True).then_inc(sums_spread, 1)

            def project(half):
                misc_free(pe, "out", half)
                pe.wait_ge(o_ready, 2 * (half + 1))
                for i in range(TPC):
                    for quad in range(H // QUAD):
                        last = nc.tensor.matmul(misc[:, D * i:D * (i + 1)],
                                                o_norm[:, 2 * half + quad, P * i:P * (i + 1)],
                                                vin_sb[:, D * (1 + quad):D * (2 + quad)],
                                                start=(quad == 0), stop=(quad == H // QUAD - 1))
                last.then_inc(projected, 1)

            for i in (0, 1, 2):
                pe.wait_ge(k_grp[i], 16)
                pe.wait_ge(q_grp[i], 16)
            for u in range(AHEAD):
                unit_scores(u)
            pe.wait_ge(consts_ready, 3)
            turn_shift(0)
            for i in (3, 4, 5):
                pe.wait_ge(k_grp[i], 16)
                pe.wait_ge(q_grp[i], 16)
            pe.wait_ge(minus_ready, 1)
            pe.wait_ge(v_ready, 1)
            pe.wait_ge(ones_ready, 1)
            for s in range(LAST + 1):
                if s < len(STEPS):
                    step_scores(s)
                for u in units_in(s):
                    unit_scores(u)
                if 0 <= s - PV_LAG < len(STEPS):
                    step_values(s - PV_LAG)
                if s in SHIFT_AT:
                    turn_shift(SHIFT_AT[s])
                if s in SUMS_AT:
                    spread_sums(SUMS_AT[s])
                if s in OUT_AT:
                    project(OUT_AT[s])


def kernel(x, adj, L0_gnn_h_neigh, L0_gnn_Wq, L0_gnn_bq, L0_gnn_Wk, L0_gnn_bk, L0_gnn_Wv, L0_gnn_bv,
           L0_gnn_Wo, L0_gnn_bo, L0_gnn_E):
    import concourse.bacc as bacc
    from concourse.bass_utils import run_bass_kernel_spmd

    x, adj = np.asarray(x), np.asarray(adj)

    def by_dim(a):
        return a.reshape(*a.shape[:-1], H, DH).swapaxes(-1, -2).reshape(a.shape)

    wo_t = np.asarray(L0_gnn_Wo).T.reshape(H // QUAD, QUAD, DH, D)
    wo = np.zeros((QUAD, COL, H // QUAD, D), wo_t.dtype)
    wo[:, :DH] = wo_t.transpose(1, 2, 0, 3)
    arrays = {
        "kin": np.concatenate([np.asarray(L0_gnn_h_neigh).T, by_dim(np.asarray(L0_gnn_Wk).T),
                               by_dim(np.asarray(L0_gnn_bk))[:, None],
                               np.asarray(L0_gnn_E).T], axis=1),
        "qin": np.concatenate([x.T, by_dim(np.asarray(L0_gnn_Wq).T), by_dim(np.asarray(L0_gnn_bq))[:, None]], axis=1),
        "vin": np.concatenate([np.asarray(L0_gnn_Wv).T, wo.reshape(P, 2 * D)], axis=1),
        "x": x,
        "bv": np.asarray(L0_gnn_bv),
        "bo": np.asarray(L0_gnn_bo),
        "adj": adj,
        "adj_t": adj.T,
    }
    arrays = {name: np.ascontiguousarray(a) for name, a in arrays.items()}
    nc = bacc.Bacc("TRN2", target_bir_lowering=False, num_devices=1)
    args = [nc.dram_tensor(name, a.shape, mybir.dt.from_np(a.dtype), kind="ExternalInput").ap()
            for name, a in arrays.items()]
    out = nc.dram_tensor("out", (BT, D), F32, kind="ExternalOutput").ap()
    attention_kernel(nc, *args, out)
    result = run_bass_kernel_spmd(nc, [arrays], core_ids=[0])
    return result.results[0]["out"]
```

```python
from contextlib import ExitStack

import numpy as np

import concourse.bass as bass
from concourse import mybir

F32 = mybir.dt.float32
BF16 = mybir.dt.bfloat16
I32 = mybir.dt.int32
ALU = mybir.AluOpType
AX = mybir.AxisListType
ACT = mybir.ActivationFunctionType

P = 128
BT = BN = 512
D = 128
H = 8
DH = D // H
NT = BN // P
QUAD = 4
HALF = BT // 2
TPH = HALF // P
COL = P // QUAD
GROUPS = [(1, 1), (1, 2), (2, 1), (2, 2), (1, 3), (3, 1)]
MAXROWS = 3 * DH
SPLIT = len(GROUPS) * DH
SCALE = 1.0 / DH ** 0.5
BIG = float(2.0 ** 100)
FLOOR = -float(2.0 ** 99)
LEAST = -float(2.0 ** 98)
TINY = 1e-30
EPS = 1e-5

CHUNKS = [(0, P, 0), (P, P, 0), (0, HALF, 1), (HALF, HALF, 0), (HALF, P, 1), (HALF + P, P, 1)]
PARTS = [(0, HALF), (HALF, P), (HALF + P, P)]
IN_PART = [3, 5, 6]
STEPS = [(c, (t,) if w == HALF else (2 * t, 2 * t + 1))
         for c, (_, w, _) in enumerate(CHUNKS) for t in range(NT * w // HALF)]
LAST_STEP = [max(s for s, (d, _) in enumerate(STEPS) if d == c) for c in range(len(CHUNKS))]
UNITS = [(c, i, g) for c, (_, w, _) in enumerate(CHUNKS) for i in range(w // P) for g in range(QUAD)]
FIRST_UNIT = [UNITS.index((c, 0, 0)) for c in range(len(CHUNKS))] + [len(UNITS)]
AHEAD = 6
FAST = 4
PV_LAG = 3
LAST = len(STEPS) + PV_LAG - 1
BY_POOL = [4, 6, 8, 10, 12]
WARM = 8
WARM_STACK = 6
WARM_UNIT = 1


def units_in(s):
    at = [min(AHEAD + 2 * n + min(n, FAST), len(UNITS)) for n in (s, s + 1)]
    return range(*at)


def shift_after(u):
    return FIRST_UNIT.index(u - 1) - 1 if u - 1 in FIRST_UNIT[1:] else None


def stages_in(s):
    stages = []
    if s == 3:
        stages.append(("mask", 1))
    if s > 0 and units_in(s - 1) and not units_in(s):
        stages.append(("shift", len(CHUNKS) - 1))
    stages += [("turn", c) for c in range(len(CHUNKS) - 1) if s == LAST_STEP[c] + PV_LAG + 1]
    at = LAST_STEP[IN_PART[0] - 1] + PV_LAG
    stages += [("back", 0)] * (s == at + 2) + [("out", 0)] * (s == at + 3)
    if s == LAST:
        stages += [("back", 1), ("turn", 5), ("out", 1), ("root", 0), ("finish", 0), ("back", 2), ("out", 2),
                   ("root", 1), ("finish", 1), ("root", 2), ("finish", 2)]
    return stages


def misc_order():
    order = [("mask", 0)] + [("shift", shift_after(u)) for u in range(AHEAD) if shift_after(u) is not None]
    for s in range(LAST + 1):
        order += [("shift", shift_after(u)) for u in units_in(s) if shift_after(u) is not None]
        order += [stage for stage in stages_in(s) if stage[0] in ("mask", "shift", "turn")]
    return order


MISC_ORDER = misc_order()


def attention_kernel(nc, kin, qin, vin, x, bv, bo, adj, out):
    with ExitStack() as ctx:
        def sb(name, shape, dt=F32):
            return ctx.enter_context(nc.sbuf_tensor(name, shape, dt))

        def psum(name, shape, dt=F32):
            return ctx.enter_context(nc.psum_tensor(name, shape, dt))

        def sem(name):
            return ctx.enter_context(nc.semaphore(name))

        ps_max = [psum(f"ps_max{i}", [P, BN]) for i in range(2)]
        ps_s = [psum(f"ps_s{i}", [P, 2, 2 * HALF]) for i in range(2)]
        ps_o = psum("ps_o", [P, 2 * HALF])
        misc = psum("misc", [P, 512])
        misc_t = misc[:].bitcast(BF16).rearrange("p (t b) -> p t b", t=NT)
        ps_k, ps_q, ps_v = ps_s[0][:, 0, :], ps_s[1][:, 0, :], ps_s[0][:, 1, :]

        kin_sb = sb("kin_sb", [P, BN + D + 3])
        qin_sb = sb("qin_sb", [P, BT + D + 1])
        vin_sb = sb("vin_sb", [P, 2 * D])
        x_sb = sb("x_sb", [P, BT // P, D])
        bv_sb = sb("bv_sb", [P, D])
        bo_sb = sb("bo_sb", [P, D])
        adj_sb = sb("adj_sb", [P, BT // P, BN], I32)
        mask_max = sb("mask_max", [P, BT // P, BN], BF16)
        mask_t = sb("mask_t", [P, NT, BT], BF16)
        msg = sb("msg", [P, BN])
        parts = sb("parts", [P, 6, BT], BF16)
        q_part, k_part = [parts[:, i, :] for i in range(3)], [parts[:, 3 + i, :] for i in range(3)]
        k_rest = sb("k_rest", [P, BN])
        q_rest = sb("q_rest", [P, BT])
        stack = sb("stack", [P, H, 2, BT], BF16)
        q_stack, k_stack = stack[:, :, 0, :], stack[:, :, 1, :]
        v_sb = sb("v_sb", [P, NT, D])
        v_ones = sb("v_ones", [P, NT, H, COL])
        ident = sb("ident", [P, P], BF16)
        ident32 = sb("ident32", [P, P])
        zeros = sb("zeros", [P, BN], BF16)
        one = sb("one", [P, 1])
        masked = sb("masked", [P, 2, BN], BF16)
        peak = sb("peak", [P, len(UNITS)])
        shift = sb("shift", [P, len(UNITS)])
        shift_part = sb("shift_part", [P, len(UNITS), 2], BF16)
        edge = sb("edge", [P, NT, BT], I32)
        probs = sb("probs", [P, len(STEPS), QUAD * HALF])
        o_sb = sb("o_sb", [P, len(CHUNKS), HALF])
        denom = sb("denom", [P, len(UNITS)])
        r_denom = sb("r_denom", [P, len(UNITS)])
        o_norm = sb("o_norm", [P, BT // P, H, DH])
        o_back = sb("o_back", [P, BT // P, P])
        xb = sb("xb", [P, BT // P, D])
        res = sb("res", [P, BT // P, D])
        stats = sb("stats", [P, BT // P, 6])
        mean_var = sb("mean_var", [P, BT // P, 2])
        eps = sb("eps", [P, 1])
        std = sb("std", [P, BT // P, 1])
        rstd = sb("rstd", [P, BT // P, 1])
        y_sb = sb("y_sb", [P, BT // P, D])

        kin_in, qin_in, vin_in = sem("kin_in"), sem("qin_in"), sem("vin_in")
        x_in, bv_in, bo_in = sem("x_in"), sem("bv_in"), sem("bo_in")
        adj_in = [sem(f"adj_in{half}") for half in range(2)]
        edge_ready, probs_masked = sem("edge_ready"), sem("probs_masked")
        stacked = [sem(f"stacked{i}") for i in range(len(GROUPS))]
        consts_ready, zeroed = sem("consts_ready"), sem("zeroed")
        ones_ready, under_zeroed, minus_ready = sem("ones_ready"), sem("under_zeroed"), sem("minus_ready")
        zeros_ready, tables_loaded = sem("zeros_ready"), sem("tables_loaded")
        msg_ready, xb_ready = sem("msg_ready"), sem("xb_ready")
        k_proj, q_proj, v_proj = sem("k_proj"), sem("q_proj"), sem("v_proj")
        k1_ready, q1_ready = sem("k1_ready"), sem("q1_ready")
        k_rest_ready, q_rest_ready = sem("k_rest_ready"), sem("q_rest_ready")
        k2_ready, q2_ready = sem("k2_ready"), sem("q2_ready")
        k3_ready, q3_ready = sem("k3_ready"), sem("q3_ready")
        v_copied, v_ready = sem("v_copied"), sem("v_ready")
        mask_max_ready = [sem(f"mask_max_ready{half}") for half in range(2)]
        mask_turned, mask_t_ready = sem("mask_turned"), sem("mask_t_ready")
        unit_scored, unit_maxed = sem("unit_scored"), sem("unit_maxed")
        shift_guarded, shift_part1, shift_ready = sem("shift_guarded"), sem("shift_part1"), sem("shift_ready")
        shift_turned, shift_in_stack = sem("shift_turned"), sem("shift_in_stack")
        step_scored, probs_ready = sem("step_scored"), sem("probs_ready")
        chunk_summed, o_copied = sem("chunk_summed"), sem("o_copied")
        o_turned, denom_ready, inverted, o_ready = sem("o_turned"), sem("denom_ready"), sem("inverted"), sem("o_ready")
        back_turned, back_ready = sem("back_turned"), sem("back_ready")
        projected, res_ready = sem("projected"), sem("res_ready")
        stats_ready, aggregated, eps_ready = sem("stats_ready"), sem("aggregated"), sem("eps_ready")
        std_ready, rstd_ready = sem("std_ready"), sem("rstd_ready")
        y_ready, y_out = sem("y_ready"), sem("y_out")

        misc_reader = {"mask": mask_t_ready, "shift": shift_in_stack, "turn": o_ready}

        def misc_free(eng, stage, n):
            at = MISC_ORDER.index((stage, n))
            if at:
                before, m = MISC_ORDER[at - 1]
                eng.wait_ge(misc_reader[before], m + 1)

        def by_head(tile, c):
            return tile.rearrange("p (t g b) -> p t g b", g=QUAD, b=CHUNKS[c][1])

        def targets(c):
            b, w, _ = CHUNKS[c]
            return slice(b, b + w)

        def tiles_of(part):
            b, w = PARTS[part]
            return slice(b // P, (b + w) // P)

        def mask_for_max(eng, half):
            eng.wait_ge(adj_in[half], 16)
            ts = slice(TPH * half, TPH * (half + 1))
            eng.tensor_scalar(mask_max[:, ts, :], adj_sb[:, ts, :], 0.0, -BIG,
                              ALU.is_equal, ALU.mult).then_inc(mask_max_ready[half], 1)

        def shift_view(c):
            w = CHUNKS[c][1]
            return misc[:].bitcast(BF16)[:, 0:QUAD * w].rearrange("p (g b) -> p g b", g=QUAD)

        w_k, b_k, e_1 = kin_sb[:, BN:BN + D], kin_sb[:, BN + D:BN + D + 1], kin_sb[:, BN + D + 2:BN + D + 3]
        w_q, b_q = qin_sb[:, BT:BT + D], qin_sb[:, BT + D:BT + D + 1]
        w_v = vin_sb[:, 0:D]

        def stack_group(eng, i):
            a, b = GROUPS[i][0] - 1, 3 + GROUPS[i][1] - 1
            eng.dma_start(stack[i * DH:(i + 1) * DH, :, :, :], parts[:, a:b + 1:b - a, :]).then_inc(stacked[i], 16)

        def load_adj(eng, half):
            eng.dma_start(adj_sb[:, TPH * half:TPH * (half + 1), :],
                          adj.rearrange("(t p) n -> p t n", p=P)[:, TPH * half:TPH * (half + 1), :]
                          ).then_inc(adj_in[half], 16)

        block = ctx.enter_context(nc.Block())

        @block.sync
        def _(sp):
            sp.dma_start(qin_sb[:], qin).then_inc(qin_in, 16)
            load_adj(sp, 0)
            sp.dma_start(vin_sb[:], vin).then_inc(vin_in, 16)
            sp.wait_ge(q1_ready, 1)
            sp.wait_ge(k1_ready, 1)
            stack_group(sp, 0)
            sp.wait_ge(q2_ready, 1)
            stack_group(sp, 2)
            sp.wait_ge(k2_ready, 1)
            stack_group(sp, 1)
            stack_group(sp, 3)
            sp.wait_ge(k3_ready, 1)
            stack_group(sp, 4)
            sp.wait_ge(q3_ready, 1)
            stack_group(sp, 5)
            load_adj(sp, 1)
            sp.dma_start(x_sb[:], x.rearrange("(t p) d -> p t d", p=P)).then_inc(x_in, 16)
            sp.dma_start(bo_sb[:], bo.partition_broadcast(P)).then_inc(bo_in, 16)
            out_v = out.rearrange("(t p) d -> p t d", p=P)
            for n in range(len(PARTS)):
                ts = tiles_of(n)
                sp.wait_ge(y_ready, ts.stop)
                sp.dma_start(out_v[:, ts, :], y_sb[:, ts, :]).then_inc(y_out, 16)
            sp.wait_ge(y_out, 16 * len(PARTS))

        @block.gpsimd
        def _(pool):
            nc.gpsimd.memset(ident[:], 0.0).then_inc(zeroed, 1)
            nc.gpsimd.memset(ident32[:], 0.0).then_inc(zeroed, 1)
            pool.wait_ge(zeroed, 2)
            for tile in (ident, ident32):
                nc.gpsimd.affine_select(out=tile[:], in_=tile[:], compare_op=ALU.not_equal, fill=1.0,
                                        base=0, pattern=[[-1, P]], channel_multiplier=1).then_inc(consts_ready, 1)
            nc.gpsimd.memset(v_ones[:, :, :, DH:COL], 1.0).then_inc(ones_ready, 1)
            pool.wait_ge(ones_ready, 1)
            nc.gpsimd.memset(stack[SPLIT:P, :, :, :].bitcast(F32), 0.0).then_inc(under_zeroed, 1)
            pool.wait_ge(under_zeroed, 1)
            nc.gpsimd.memset(k_stack[SPLIT:SPLIT + 2, :, :], -1.0).then_inc(minus_ready, 1)
            pool.wait_ge(minus_ready, 1)
            pool.wait_ge(bv_in, 16)
            pool.wait_ge(v_copied, 1)
            nc.gpsimd.tensor_tensor(v_ones[:, :, :, 0:DH], v_sb[:].rearrange("p t (h d) -> p t h d", h=H),
                                    bv_sb[:].rearrange("p (o h d) -> p o h d", o=1, h=H)
                                            .broadcast_to([P, NT, H, DH]),
                                    ALU.add).then_inc(v_ready, 1)
            def mask_probs(s):
                c, tiles = STEPS[s]
                pool.wait_ge(edge_ready, CHUNKS[c][0] // HALF + 1)
                pool.wait_ge(probs_ready, s + 1)
                p = by_head(probs[:, s, :], c).bitcast(I32)
                on = edge[:, tiles[0]:tiles[-1] + 1, targets(c)].rearrange("p t (o b) -> p t o b", o=1)
                on = on.broadcast_to(list(p.shape))
                nc.gpsimd.tensor_tensor(p, p, on, ALU.mult).then_inc(probs_masked, 1)

            mask_for_max(nc.gpsimd, 1)
            for s in BY_POOL:
                mask_probs(s)
            pool.wait_ge(x_in, 16)
            pool.wait_ge(bo_in, 16)
            for t in range(BT // P):
                nc.gpsimd.tensor_tensor(xb[:, t, :], x_sb[:, t, :], bo_sb[:], ALU.add).then_inc(xb_ready, 1)

        @block.scalar
        def _(act):
            act.dma_start(kin_sb[:], kin).then_inc(kin_in, 16)
            act.dma_start(bv_sb[:], bv.partition_broadcast(P)).then_inc(bv_in, 16)
            act.wait_ge(zeros_ready, 1)
            nc.scalar.activation(one[:], zeros[:, 0:1], ACT.Exp).then_inc(tables_loaded, 1)
            act.wait_ge(q_proj, 1)
            nc.scalar.activation(q_part[0], ps_q, ACT.Identity, bias=b_q).then_inc(q1_ready, 1)
            act.wait_ge(k_proj, 1)
            nc.scalar.activation(k_part[0], ps_k, ACT.Identity, bias=b_k).then_inc(k1_ready, 1)
            act.wait_ge(v_proj, 1)
            nc.scalar.activation(v_sb[:], ps_v, ACT.Copy).then_inc(v_copied, 1)

            def mask_rows(half):
                act.wait_ge(mask_turned, half + 1)
                bs = slice(HALF * half, HALF * (half + 1))
                nc.scalar.activation(mask_t[:, :, bs], misc_t, ACT.Copy).then_inc(mask_t_ready, 1)

            def edges(half):
                act.wait_ge(mask_t_ready, half + 1)
                bs = slice(HALF * half, HALF * (half + 1))
                nc.scalar.activation(edge[:, :, bs], mask_t[:, :, bs], ACT.Copy, bias=1.0,
                                     scale=1.0 / BIG).then_inc(edge_ready, 1)

            def shift_rows(c):
                quad = CHUNKS[c][2]
                act.wait_ge(shift_turned, c + 1)
                nc.scalar.activation(q_stack[SPLIT:SPLIT + 2, QUAD * quad:QUAD * (quad + 1), targets(c)],
                                     shift_view(c)[SPLIT:SPLIT + 2, :, :], ACT.Copy).then_inc(shift_in_stack, 1)

            def copy_o(c):
                act.wait_ge(chunk_summed, c + 1)
                w = CHUNKS[c][1]
                nc.scalar.activation(o_sb[:, c, 0:w], ps_o[:, 0:w], ACT.Copy).then_inc(o_copied, 1)

            def copy_back(part):
                act.wait_ge(back_turned, part + 1)
                nc.scalar.activation(o_back[:, tiles_of(part), :], ps_max[0][:, 0:PARTS[part][1]],
                                     ACT.Copy).then_inc(back_ready, 1)

            def deviation(part):
                act.wait_ge(eps_ready, 1)
                act.wait_ge(aggregated, tiles_of(part).stop)
                nc.scalar.activation(std[:, tiles_of(part), :], mean_var[:, tiles_of(part), 1:2], ACT.Sqrt,
                                     bias=eps[:]).then_inc(std_ready, 1)

            mask_rows(0)
            edges(0)
            shift_rows(0)
            for s in range(LAST + 1):
                if s < len(STEPS):
                    act.wait_ge(step_scored, s + 1)
                    nc.scalar.activation(probs[:, s, :], ps_s[s % 2][:], ACT.Exp, scale=SCALE).then_inc(probs_ready, 1)
                if s - PV_LAG in LAST_STEP:
                    copy_o(LAST_STEP.index(s - PV_LAG))
                for u in units_in(s):
                    if shift_after(u) is not None:
                        shift_rows(shift_after(u))
                for stage, n in stages_in(s):
                    if stage == "mask":
                        mask_rows(n)
                        edges(n)
                    if stage == "shift":
                        shift_rows(n)
                    if stage == "back":
                        copy_back(n)
                    if stage == "root":
                        deviation(n)

        @block.vector
        def _(dve):
            nc.vector.memset(zeros[:], 0.0).then_inc(zeros_ready, 1)
            nc.vector.memset(eps[:], EPS).then_inc(eps_ready, 1)
            dve.wait_ge(kin_in, 16)
            nc.vector.tensor_scalar(msg[:], kin_sb[:, 0:BN], e_1, None, ALU.add).then_inc(msg_ready, 1)

            def rest(proj, bias, part, out_, first, done):
                dve.wait_ge(first, 1)
                nc.vector.scalar_tensor_tensor(out=out_[:], in0=proj, scalar=bias,
                                               in1=part[0], op0=ALU.add, op1=ALU.subtract).then_inc(done, 1)

            rest(ps_q, b_q, q_part, q_rest, q1_ready, q_rest_ready)
            dve.wait_ge(q_rest_ready, 1)
            nc.vector.tensor_copy(q_part[1], q_rest[:]).then_inc(q2_ready, 1)
            rest(ps_k, b_k, k_part, k_rest, k1_ready, k_rest_ready)
            dve.wait_ge(k_rest_ready, 1)
            nc.vector.tensor_copy(k_part[1], k_rest[:]).then_inc(k2_ready, 1)
            dve.wait_ge(q2_ready, 1)
            nc.vector.tensor_tensor(q_part[2], q_rest[:], q_part[1], ALU.subtract).then_inc(q3_ready, 1)
            dve.wait_ge(k2_ready, 1)
            nc.vector.tensor_tensor(k_part[2], k_rest[:], k_part[1], ALU.subtract).then_inc(k3_ready, 1)
            mask_for_max(nc.vector, 0)

            def unit_max(u):
                c, i, g = UNITS[u]
                b = CHUNKS[c][0] // P + i
                dve.wait_ge(mask_max_ready[b // TPH], 1)
                dve.wait_ge(unit_scored, u + 1)
                if u >= 2:
                    dve.wait_ge(unit_maxed, u - 1)
                nc.vector.tensor_tensor_reduce(masked[:, u % 2, :], ps_max[u % 2][:],
                                               mask_max[:, b, :], 1.0, FLOOR,
                                               ALU.add, ALU.max, peak[:, u:u + 1]).then_inc(unit_maxed, 1)
                if u + 1 in FIRST_UNIT:
                    shift_parts(c)

            def shift_parts(c):
                us = slice(FIRST_UNIT[c], FIRST_UNIT[c + 1])
                dve.wait_ge(unit_maxed, FIRST_UNIT[c + 1])
                nc.vector.scalar_tensor_tensor(out=shift[:, us], in0=peak[:, us], scalar=LEAST, in1=peak[:, us],
                                               op0=ALU.is_gt, op1=ALU.mult).then_inc(shift_guarded, 1)
                dve.wait_ge(shift_guarded, c + 1)
                nc.vector.tensor_copy(shift_part[:, us, 0], shift[:, us]).then_inc(shift_part1, 1)
                dve.wait_ge(shift_part1, c + 1)
                nc.vector.tensor_tensor(shift_part[:, us, 1], shift[:, us], shift_part[:, us, 0],
                                        ALU.subtract).then_inc(shift_ready, 1)

            def normalise(c):
                b, w, quad = CHUNKS[c]
                us = slice(FIRST_UNIT[c], FIRST_UNIT[c + 1])
                turned = misc[:, 0:w].rearrange("p (i g j) -> p i g j", i=w // P, g=QUAD)
                dve.wait_ge(o_turned, c + 1)
                nc.vector.tensor_scalar(denom[:, us], turned[:, :, :, DH:DH + 1], TINY, None,
                                        ALU.max).then_inc(denom_ready, 1)
                dve.wait_ge(denom_ready, c + 1)
                nc.vector.reciprocal(r_denom[:, us], denom[:, us]).then_inc(inverted, 1)
                dve.wait_ge(inverted, c + 1)
                out_ = o_norm[:, b // P:(b + w) // P, QUAD * quad:QUAD * (quad + 1), :]
                nc.vector.tensor_tensor(out_, turned[:, :, :, 0:DH],
                                        r_denom[:, us].rearrange("p (i g o) -> p i g o", i=w // P, o=1)
                                                      .broadcast_to(list(out_.shape)), ALU.mult).then_inc(o_ready, 1)

            def residual(part):
                ts = tiles_of(part)
                dve.wait_ge(projected, part + 1)
                dve.wait_ge(xb_ready, BT // P)
                nc.vector.tensor_tensor(res[:, ts, :], ps_max[1][:, 0:PARTS[part][1]].rearrange(
                    "p (t d) -> p t d", d=D), xb[:, ts, :], ALU.add).then_inc(res_ready, 1)
                dve.wait_ge(res_ready, part + 1)
                for t in range(ts.start, ts.stop):
                    nc.vector.bn_stats(stats[:, t, :], res[:, t, :]).then_inc(stats_ready, 1)
                for t in range(ts.start, ts.stop):
                    dve.wait_ge(stats_ready, t + 1)
                    nc.vector.bn_aggr(mean_var[:, t, :], stats[:, t, :]).then_inc(aggregated, 1)

            def finish(part):
                ts = tiles_of(part)
                dve.wait_ge(std_ready, part + 1)
                nc.vector.reciprocal(rstd[:, ts, :], std[:, ts, :]).then_inc(rstd_ready, 1)
                dve.wait_ge(rstd_ready, part + 1)
                for t in range(ts.start, ts.stop):
                    nc.vector.tensor_scalar(y_sb[:, t, :], res[:, t, :], mean_var[:, t, 0:1], rstd[:, t, :],
                                            ALU.subtract, ALU.mult).then_inc(y_ready, 1)

            for u in range(AHEAD):
                unit_max(u)
            for s in range(LAST + 1):
                for u in units_in(s):
                    unit_max(u)
                for stage, n in stages_in(s):
                    if stage == "turn":
                        normalise(n)
                    if stage == "out":
                        residual(n)
                    if stage == "finish":
                        finish(n)

        @block.tensor
        def _(pe):
            def keep_warm(n):
                for _ in range(n):
                    nc.tensor.matmul(ps_o[:], zeros[:, 0:P], zeros[:], start=True, stop=True)

            pe.wait_ge(zeros_ready, 1)
            keep_warm(WARM)
            pe.wait_ge(qin_in, 16)
            nc.tensor.matmul(ps_q, w_q, qin_sb[:, 0:BT], start=True, stop=True).then_inc(q_proj, 1)
            pe.wait_ge(msg_ready, 1)
            nc.tensor.matmul(ps_k, w_k, msg[:], start=True, stop=True).then_inc(k_proj, 1)
            pe.wait_ge(vin_in, 16)
            v_out = ps_v.rearrange("p (t d) -> p t d", t=NT)
            for t in range(NT):
                last = nc.tensor.matmul(v_out[:, t, :], msg[:, t * P:(t + 1) * P], w_v, start=True, stop=True)
            last.then_inc(v_proj, 1)

            def turn_mask(half):
                pe.wait_ge(mask_max_ready[half], 1)
                misc_free(pe, "mask", half)
                for i in range(TPH):
                    for t in range(NT):
                        last = nc.tensor.transpose(misc_t[:, t, P * i:P * (i + 1)],
                                                   mask_max[:, TPH * half + i, P * t:P * (t + 1)], ident[:])
                last.then_inc(mask_turned, 1)

            def unit_scores(u):
                c, i, g = UNITS[u]
                b0, _, quad = CHUNKS[c]
                h, b = QUAD * quad + g, b0 + P * i
                rows = MAXROWS if c == 0 else P
                if u >= 2:
                    pe.wait_ge(unit_maxed, u - 1)
                nc.tensor.matmul(ps_max[u % 2][:], q_stack[0:rows, h, b:b + P], k_stack[0:rows, h, :],
                                 start=True, stop=True).then_inc(unit_scored, 1)
                if shift_after(u) is not None:
                    turn_shift(shift_after(u))

            def turn_shift(c):
                pe.wait_ge(shift_ready, c + 1)
                misc_free(pe, "shift", c)
                for u in range(FIRST_UNIT[c], FIRST_UNIT[c + 1]):
                    _, i, g = UNITS[u]
                    last = nc.tensor.transpose(shift_view(c)[SPLIT:SPLIT + 2, g, P * i:P * (i + 1)],
                                               shift_part[:, u, :], ident[:])
                last.then_inc(shift_turned, 1)

            def step_scores(s):
                c, tiles = STEPS[s]
                b, w, quad = CHUNKS[c]
                pe.wait_ge(shift_in_stack, c + 1)
                if s >= 2:
                    pe.wait_ge(probs_ready, s - 1)
                pe.wait_ge(mask_t_ready, b // HALF + 1)
                scores = ps_s[s % 2]
                for bank in range(2):
                    t = tiles[bank % len(tiles)]
                    heads = range(2 * bank, 2 * bank + 2) if w == HALF else range(QUAD)
                    if s not in BY_POOL:
                        mask = mask_t[:, t, targets(c)].rearrange("p (o b) -> p o b", o=1)
                        nc.tensor.matmul(scores[:, bank, :], ident[:], mask.broadcast_to([P, len(heads), w]),
                                         start=True, stop=False, skip_group_check=True)
                    for n, g in enumerate(heads):
                        h = QUAD * quad + g
                        last = nc.tensor.matmul(scores[:, bank, w * n:w * (n + 1)], k_stack[:, h, t * P:(t + 1) * P],
                                                q_stack[:, h, targets(c)], start=s in BY_POOL, stop=True,
                                                skip_group_check=True)
                last.then_inc(step_scored, 1)

            def step_values(s):
                c, tiles = STEPS[s]
                _, w, quad = CHUNKS[c]
                if c >= 1 and STEPS[s - 1][0] != c:
                    pe.wait_ge(o_copied, c)
                if s in BY_POOL:
                    pe.wait_ge(probs_masked, BY_POOL.index(s) + 1)
                else:
                    pe.wait_ge(probs_ready, s + 1)
                p = by_head(probs[:, s, :], c)
                for n, t in enumerate(tiles):
                    for g in range(QUAD):
                        last = nc.tensor.matmul(ps_o[COL * g:COL * (g + 1), 0:w], v_ones[:, t, QUAD * quad + g, :],
                                                p[:, n, g, :], start=(t == 0), stop=(t == NT - 1))
                if t == NT - 1:
                    last.then_inc(chunk_summed, 1)

            def turn_o(c):
                misc_free(pe, "turn", c)
                pe.wait_ge(o_copied, c + 1)
                for i in range(CHUNKS[c][1] // P):
                    last = nc.tensor.transpose(misc[:, P * i:P * (i + 1)], o_sb[:, c, P * i:P * (i + 1)], ident32[:])
                last.then_inc(o_turned, 1)

            def turn_back(part):
                pe.wait_ge(o_ready, IN_PART[part])
                pe.wait_ge(unit_maxed, len(UNITS))
                if part:
                    pe.wait_ge(back_ready, part)
                for i, t in enumerate(range(tiles_of(part).start, tiles_of(part).stop)):
                    last = nc.tensor.transpose(ps_max[0][:, P * i:P * (i + 1)],
                                               o_norm[:, t, :, :].rearrange("p h d -> p (h d)"), ident32[:])
                last.then_inc(back_turned, 1)

            def project(part):
                pe.wait_ge(back_ready, part + 1)
                if part:
                    pe.wait_ge(res_ready, part)
                for i, t in enumerate(range(tiles_of(part).start, tiles_of(part).stop)):
                    last = nc.tensor.matmul(ps_max[1][:, D * i:D * (i + 1)], o_back[:, t, :],
                                            vin_sb[:, D:2 * D], start=True, stop=True)
                last.then_inc(projected, 1)

            pe.wait_ge(consts_ready, 2)
            turn_mask(0)
            keep_warm(WARM_STACK)
            pe.wait_ge(under_zeroed, 1)
            pe.wait_ge(minus_ready, 1)
            for i in range(len(GROUPS)):
                pe.wait_ge(stacked[i], 16)
                if i == 2:
                    for u in range(FIRST_UNIT[1]):
                        unit_scores(u)
                        keep_warm(WARM_UNIT)
            for u in range(FIRST_UNIT[1], AHEAD):
                unit_scores(u)
                keep_warm(WARM_UNIT)
            pe.wait_ge(v_ready, 1)
            pe.wait_ge(ones_ready, 1)
            for s in range(LAST + 1):
                if s < len(STEPS):
                    step_scores(s)
                for u in units_in(s):
                    unit_scores(u)
                if 0 <= s - PV_LAG < len(STEPS):
                    step_values(s - PV_LAG)
                for stage, n in stages_in(s):
                    if stage == "mask":
                        turn_mask(n)
                    if stage == "shift":
                        turn_shift(n)
                    if stage == "turn":
                        turn_o(n)
                    if stage == "back":
                        turn_back(n)
                    if stage == "out":
                        project(n)


def kernel(x, adj, L0_gnn_h_neigh, L0_gnn_Wq, L0_gnn_bq, L0_gnn_Wk, L0_gnn_bk, L0_gnn_Wv, L0_gnn_bv,
           L0_gnn_Wo, L0_gnn_bo, L0_gnn_E):
    import concourse.bacc as bacc
    from concourse.bass_utils import run_bass_kernel_spmd

    x, adj = np.asarray(x), np.asarray(adj)

    def by_dim(a):
        return a.reshape(*a.shape[:-1], H, DH).swapaxes(-1, -2).reshape(a.shape)

    arrays = {
        "kin": np.concatenate([np.asarray(L0_gnn_h_neigh).T, by_dim(np.asarray(L0_gnn_Wk).T),
                               by_dim(np.asarray(L0_gnn_bk))[:, None],
                               np.asarray(L0_gnn_E).T], axis=1),
        "qin": np.concatenate([x.T, by_dim(np.asarray(L0_gnn_Wq).T), by_dim(np.asarray(L0_gnn_bq))[:, None]], axis=1),
        "vin": np.concatenate([np.asarray(L0_gnn_Wv).T, np.asarray(L0_gnn_Wo).T], axis=1),
        "x": x,
        "bv": np.asarray(L0_gnn_bv),
        "bo": np.asarray(L0_gnn_bo),
        "adj": adj,
    }
    arrays = {name: np.ascontiguousarray(a) for name, a in arrays.items()}
    nc = bacc.Bacc("TRN2", target_bir_lowering=False, num_devices=1)
    args = [nc.dram_tensor(name, a.shape, mybir.dt.from_np(a.dtype), kind="ExternalInput").ap()
            for name, a in arrays.items()]
    out = nc.dram_tensor("out", (BT, D), F32, kind="ExternalOutput").ap()
    attention_kernel(nc, *args, out)
    result = run_bass_kernel_spmd(nc, [arrays], core_ids=[0])
    return result.results[0]["out"]
```

```python
from contextlib import ExitStack

import numpy as np

import concourse.bass as bass
from concourse import mybir

F32 = mybir.dt.float32
BF16 = mybir.dt.bfloat16
I32 = mybir.dt.int32
ALU = mybir.AluOpType
AX = mybir.AxisListType
ACT = mybir.ActivationFunctionType

P = 128
BT = BN = 512
D = 128
H = 8
DH = D // H
NT = BN // P
QUAD = 4
HALF = BT // 2
TPH = HALF // P
COL = P // QUAD
GROUPS = [(1, 1), (1, 2), (2, 1), (2, 2), (1, 3), (3, 1)]
MAXROWS = 3 * DH
SPLIT = len(GROUPS) * DH
ROWS = SPLIT + 2
SCALE = 1.0 / DH ** 0.5
BIG = float(2.0 ** 100)
FLOOR = -float(2.0 ** 99)
LEAST = -float(2.0 ** 98)
TINY = 1e-30
EPS = 1e-5

CHUNKS = [(0, P, 0), (P, P, 0), (0, HALF, 1), (HALF, HALF, 0), (HALF, P, 1), (HALF + P, P, 1)]
PARTS = [(0, HALF), (HALF, P), (HALF + P, P)]
IN_PART = [3, 5, 6]
STEPS = [(c, (t,) if w == HALF else (2 * t, 2 * t + 1))
         for c, (_, w, _) in enumerate(CHUNKS) for t in range(NT * w // HALF)]
LAST_STEP = [max(s for s, (d, _) in enumerate(STEPS) if d == c) for c in range(len(CHUNKS))]
UNITS = [(c, i, g) for c, (_, w, _) in enumerate(CHUNKS) for i in range(w // P) for g in range(QUAD)]
FIRST_UNIT = [UNITS.index((c, 0, 0)) for c in range(len(CHUNKS))] + [len(UNITS)]

AHEAD = 8
UNITS_AT = [2, 3, 3, 3, 2, 2, 3, 2, 1, 3, 0, 0]
SHIFT_FIRST = [1, 2, 4]
PE_ORDER = ["0u1uvu", "0uv1u", "0u1uvu", "vu0u1", "u01uv", "0u1uvu", "0u1uvu", "01uv",
            "01uv", "0u1uvu", "01uuv", "01vuu", "01uv", "v01uu", "01uuv", "0uv1u"]
PV_LAG = 3
LAST = len(STEPS) + PV_LAG - 1
BY_POOL = [1, 3, 4, 5, 7, 9]
BY_DVE = [10, 11, 12, 13]
O_BY_DVE = [2, 4, 5]
BACK_BY_DVE = [1]
END = [("back", 1), ("turn", 5), ("out", 1), ("back", 2), ("finish", 0),
       ("stats", 1), ("out", 2), ("root", 1), ("stats", 2), ("finish", 1),
       ("finish", 2), ("root", 2)]
CAP_IN = 5
MASK_IN = 4
WARM = 8
WARM_UNIT = 1


def units_in(s):
    at = AHEAD + sum(UNITS_AT[:s])
    return range(at, at + (UNITS_AT[s] if s < len(UNITS_AT) else 0))


def shift_after(u):
    return FIRST_UNIT.index(u - 1) - 1 if u - 1 in FIRST_UNIT[1:] else None


def stages_in(s):
    stages = []
    if s == MASK_IN:
        stages.append(("mask", 1))
    if s == CAP_IN:
        stages.append(("cap", 1))
    if s > 0 and units_in(s - 1) and not units_in(s):
        stages.append(("shift", len(CHUNKS) - 1))
    stages += [("turn", c) for c in range(len(CHUNKS) - 1) if s == LAST_STEP[c] + PV_LAG + 1]
    at = LAST_STEP[IN_PART[0] - 1] + PV_LAG
    stages += [("back", 0)] * (s == at + 2) + [("out", 0), ("stats", 0)] * (s == at + 3)
    stages += [("root", 0)] * (s == len(STEPS) - 1)
    if s == LAST:
        stages += END
    return stages


def misc_order():
    order = [("mask", 0)] + [("shift", shift_after(u)) for u in range(AHEAD) if shift_after(u) is not None]
    for s in range(LAST + 1):
        order += [("shift", shift_after(u)) for u in units_in(s) if shift_after(u) is not None]
        order += [stage for stage in stages_in(s) if stage[0] in ("mask", "shift", "turn")]
    order.remove(("turn", len(CHUNKS) - 1))
    return order


MISC_ORDER = misc_order()


def attention_kernel(nc, kin, qin, vin, x, bv, bo, adj, out):
    with ExitStack() as ctx:
        def sb(name, shape, dt=F32):
            return ctx.enter_context(nc.sbuf_tensor(name, shape, dt))

        def psum(name, shape, dt=F32):
            return ctx.enter_context(nc.psum_tensor(name, shape, dt))

        def sem(name):
            return ctx.enter_context(nc.semaphore(name))

        ps_max = [psum(f"ps_max{i}", [P, BN]) for i in range(2)]
        ps_s = [psum(f"ps_s{i}", [P, 2, 2 * HALF]) for i in range(2)]
        ps_o = psum("ps_o", [P, 2 * HALF])
        misc = psum("misc", [P, 512])
        misc_t = misc[:].bitcast(BF16).rearrange("p (t b) -> p t b", t=NT)
        ps_k, ps_q, ps_v = ps_s[0][:, 0, :], ps_s[1][:, 0, :], ps_s[0][:, 1, :]

        kin_sb = sb("kin_sb", [P, BN + D + 3])
        qin_sb = sb("qin_sb", [P, BT + D + 1])
        vin_sb = sb("vin_sb", [P, 2 * D])
        x_sb = sb("x_sb", [P, BT // P, D])
        bv_sb = sb("bv_sb", [P, D])
        bo_sb = sb("bo_sb", [P, D])
        adj_sb = sb("adj_sb", [P, BT // P, BN], I32)
        mask_max = sb("mask_max", [P, BT // P, BN], BF16)
        mask_t = sb("mask_t", [P, NT, BT], BF16)
        msg = sb("msg", [P, BN])
        parts = sb("parts", [P, 6, BT], BF16)
        q_part, k_part = [parts[:, i, :] for i in range(3)], [parts[:, 3 + i, :] for i in range(3)]
        head_sums = sb("head_sums", [P, QUAD])
        head_rows = sb("head_rows", [P, QUAD], BF16)
        q_heads = sb("q_heads", [P, 2, QUAD, P], BF16)
        k_rest = sb("k_rest", [P, BN])
        q_rest = sb("q_rest", [P, BT])
        stack = sb("stack", [P, H, 2, BT], BF16)
        q_stack, k_stack = stack[:, :, 0, :], stack[:, :, 1, :]
        v_sb = sb("v_sb", [P, NT, D])
        v_ones = sb("v_ones", [P, NT, H, COL])
        ident = sb("ident", [P, P], BF16)
        ident32 = sb("ident32", [P, P])
        zeros = sb("zeros", [P, BN], BF16)
        one = sb("one", [P, 1])
        masked = sb("masked", [P, 2, BN], BF16)
        peak = sb("peak", [P, len(UNITS)])
        peak1 = sb("peak1", [P, len(UNITS)], BF16)
        shift_part = sb("shift_part", [P, len(UNITS), 2], BF16)
        edge = sb("edge", [P, NT, BT], I32)
        cap = sb("cap", [P, NT, BT], BF16)
        probs = sb("probs", [P, len(STEPS), QUAD * HALF])
        o_sb = sb("o_sb", [P, len(CHUNKS), HALF])
        r_denom = sb("r_denom", [P, len(UNITS)])
        o_norm = sb("o_norm", [P, BT // P, H, DH])
        o_back = sb("o_back", [P, BT // P, P])
        xb = sb("xb", [P, BT // P, D])
        res = sb("res", [P, BT // P, D])
        stats = sb("stats", [P, BT // P, 6])
        mean_var = sb("mean_var", [P, BT // P, 2])
        eps = sb("eps", [P, 1])
        guard = sb("guard", [P, 1])
        std = sb("std", [P, BT // P, 1])
        rstd = sb("rstd", [P, BT // P, 1])
        y_sb = sb("y_sb", [P, BT // P, D])

        kin_in, qin_in, vin_in = sem("kin_in"), sem("qin_in"), sem("vin_in")
        x_in, bv_in, bo_in = sem("x_in"), sem("bv_in"), sem("bo_in")
        adj_in = [sem(f"adj_in{half}") for half in range(2)]
        edge_ready, cap_ready = sem("edge_ready"), sem("cap_ready")
        pool_masked, dve_masked = sem("pool_masked"), sem("dve_masked")
        stacked = [[sem(f"stacked{quad}_{i}") for i in range(len(GROUPS))] for quad in range(2)]
        consts_ready, zeroed = sem("consts_ready"), sem("zeroed")
        ones_ready, minus_ready = sem("ones_ready"), sem("minus_ready")
        guard_set, guard_ready = sem("guard_set"), sem("guard_ready")
        zeros_ready, tables_loaded = sem("zeros_ready"), sem("tables_loaded")
        msg_ready, xb_ready = sem("msg_ready"), sem("xb_ready")
        k_proj, q_proj, v_proj = sem("k_proj"), sem("q_proj"), sem("v_proj")
        k1_ready, q1_ready = sem("k1_ready"), sem("q1_ready")
        k_rest_ready, q_rest_ready = sem("k_rest_ready"), sem("q_rest_ready")
        k2_ready, q2_ready = sem("k2_ready"), sem("q2_ready")
        head_summed = sem("head_summed")
        head_rows_ready, q_heads_ready = sem("head_rows_ready"), [sem(f"q_heads{i}_ready") for i in range(2)]
        k3_ready, q3_ready = sem("k3_ready"), sem("q3_ready")
        v_copied, v_ready = sem("v_copied"), sem("v_ready")
        mask_max_ready = [sem(f"mask_max_ready{half}") for half in range(2)]
        mask_turned, mask_t_ready = sem("mask_turned"), sem("mask_t_ready")
        unit_scored, unit_maxed = sem("unit_scored"), sem("unit_maxed")
        shift_part1, shift_guarded, shift_ready = sem("shift_part1"), sem("shift_guarded"), sem("shift_ready")
        shift_turned, shift_in_stack = sem("shift_turned"), sem("shift_in_stack")
        step_scored, probs_ready = sem("step_scored"), sem("probs_ready")
        chunk_summed, o_copied = sem("chunk_summed"), [sem(f"o_copied{c}") for c in range(len(CHUNKS))]
        o_turned, inverted, o_ready = sem("o_turned"), sem("inverted"), sem("o_ready")
        back_turned, back_ready = sem("back_turned"), [sem(f"back_ready{part}") for part in range(len(PARTS))]
        projected, res_ready = sem("projected"), sem("res_ready")
        stats_ready, aggregated, eps_ready = sem("stats_ready"), sem("aggregated"), sem("eps_ready")
        std_ready, rstd_ready = sem("std_ready"), sem("rstd_ready")
        y_ready, y_out = sem("y_ready"), sem("y_out")

        misc_reader = {"mask": mask_t_ready, "shift": shift_in_stack, "turn": o_ready}

        def misc_free(eng, stage, n):
            at = MISC_ORDER.index((stage, n))
            if at:
                before, m = MISC_ORDER[at - 1]
                eng.wait_ge(misc_reader[before], m + 1)

        def by_head(tile, c):
            return tile.rearrange("p (t g b) -> p t g b", g=QUAD, b=CHUNKS[c][1])

        def targets(c):
            b, w, _ = CHUNKS[c]
            return slice(b, b + w)

        def tiles_of(part):
            b, w = PARTS[part]
            return slice(b // P, (b + w) // P)

        def mask_for_max(eng, half):
            eng.wait_ge(adj_in[half], 16)
            ts = slice(TPH * half, TPH * (half + 1))
            eng.tensor_scalar(mask_max[:, ts, :], adj_sb[:, ts, :], 0.0, -BIG,
                              ALU.is_equal, ALU.mult).then_inc(mask_max_ready[half], 1)

        def sums_of(c):
            return {3: ps_max[0][:], 5: ps_s[0][:, 0, :]}.get(c, ps_o[:])

        def turned_of(c):
            return misc[:] if c < len(CHUNKS) - 1 else ps_s[1][:, 1, :]

        def back_of(part):
            return ps_max[1][:, 0:HALF] if part < len(PARTS) - 1 else ps_s[0][:, 1, :]

        def out_of(part):
            return ps_max[1][:, HALF:2 * HALF] if part < len(PARTS) - 1 else ps_s[1][:, 0, :]

        def copy_o(eng, c):
            eng.wait_ge(guard_ready, QUAD)
            eng.wait_ge(chunk_summed, c + 1)
            w = CHUNKS[c][1]
            out_, in_ = o_sb[:, c, 0:w], sums_of(c)[:, 0:w]
            if c in O_BY_DVE:
                nc.vector.tensor_scalar(out_, in_, guard[:], None, ALU.add).then_inc(o_copied[c], 1)
            else:
                nc.scalar.activation(out_, in_, ACT.Identity, bias=guard[:]).then_inc(o_copied[c], 1)

        def copy_back(eng, part):
            eng.wait_ge(back_turned, part + 1)
            out_, in_ = o_back[:, tiles_of(part), :], back_of(part)[:, 0:PARTS[part][1]]
            if part in BACK_BY_DVE:
                nc.vector.tensor_copy(out_, in_.rearrange("p (t b) -> p t b", b=P)).then_inc(back_ready[part], 1)
            else:
                nc.scalar.activation(out_, in_, ACT.Copy).then_inc(back_ready[part], 1)

        def shift_view(c):
            w = CHUNKS[c][1]
            return misc[:].bitcast(BF16)[:, 0:QUAD * w].rearrange("p (g b) -> p g b", g=QUAD)

        w_k, b_k, e_1 = kin_sb[:, BN:BN + D], kin_sb[:, BN + D:BN + D + 1], kin_sb[:, BN + D + 2:BN + D + 3]
        w_q, b_q = qin_sb[:, BT:BT + D], qin_sb[:, BT + D:BT + D + 1]
        w_v = vin_sb[:, 0:D]

        def stack_group(eng, quad, i):
            a, b = GROUPS[i][0] - 1, 3 + GROUPS[i][1] - 1
            eng.dma_start(stack[i * DH:(i + 1) * DH, QUAD * quad:QUAD * (quad + 1), :, :],
                          parts[quad * D // 2:(quad + 1) * D // 2, a:b + 1:b - a, :]).then_inc(stacked[quad][i], 16)

        def single_heads(eng, part):
            eng.wait_ge(head_rows_ready, 1)
            out_ = q_heads[:, part, :, :]
            eng.tensor_tensor(out_, q_part[part][:, 0:P].rearrange("p (o b) -> p o b", o=1).broadcast_to([P, QUAD, P]),
                              head_rows[:].rearrange("p (g o) -> p g o", o=1).broadcast_to([P, QUAD, P]),
                              ALU.mult).then_inc(q_heads_ready[part], 1)

        def third_part(eng, rest, part, rest_ready, part2_ready, done):
            eng.wait_ge(rest_ready, 1)
            eng.wait_ge(part2_ready, 1)
            eng.tensor_tensor(part[2], rest[:], part[1], ALU.subtract).then_inc(done, 1)

        def load_adj(eng, half):
            eng.dma_start(adj_sb[:, TPH * half:TPH * (half + 1), :],
                          adj.rearrange("(t p) n -> p t n", p=P)[:, TPH * half:TPH * (half + 1), :]
                          ).then_inc(adj_in[half], 16)

        block = ctx.enter_context(nc.Block())

        @block.sync
        def _(sp):
            sp.dma_start(qin_sb[:], qin).then_inc(qin_in, 16)
            load_adj(sp, 0)
            sp.dma_start(vin_sb[:], vin).then_inc(vin_in, 16)
            sp.wait_ge(q1_ready, 1)
            sp.wait_ge(k1_ready, 1)
            stack_group(sp, 0, 0)
            sp.wait_ge(q2_ready, 1)
            stack_group(sp, 0, 2)
            sp.wait_ge(k2_ready, 1)
            stack_group(sp, 0, 1)
            stack_group(sp, 0, 3)
            stack_group(sp, 1, 1)
            sp.wait_ge(k3_ready, 1)
            stack_group(sp, 0, 4)
            stack_group(sp, 1, 3)
            sp.wait_ge(q3_ready, 1)
            stack_group(sp, 0, 5)
            stack_group(sp, 1, 4)
            stack_group(sp, 1, 5)
            load_adj(sp, 1)
            sp.dma_start(x_sb[:], x.rearrange("(t p) d -> p t d", p=P)).then_inc(x_in, 16)
            sp.dma_start(bo_sb[:], bo.partition_broadcast(P)).then_inc(bo_in, 16)
            out_v = out.rearrange("(t p) d -> p t d", p=P)
            for n in range(len(PARTS)):
                ts = tiles_of(n)
                sp.wait_ge(y_ready, ts.stop)
                sp.dma_start(out_v[:, ts, :], y_sb[:, ts, :]).then_inc(y_out, 16)
            sp.wait_ge(y_out, 16 * len(PARTS))

        @block.gpsimd
        def _(pool):
            nc.gpsimd.memset(ident[:], 0.0).then_inc(zeroed, 1)
            nc.gpsimd.memset(ident32[:], 0.0).then_inc(zeroed, 1)
            pool.wait_ge(zeroed, 2)
            for tile in (ident, ident32):
                nc.gpsimd.affine_select(out=tile[:], in_=tile[:], compare_op=ALU.not_equal, fill=1.0,
                                        base=0, pattern=[[-1, P]], channel_multiplier=1).then_inc(consts_ready, 1)
            nc.gpsimd.memset(v_ones[:, :, :, DH:COL], 1.0).then_inc(ones_ready, 1)
            pool.wait_ge(ones_ready, 1)
            nc.gpsimd.memset(k_stack[SPLIT:SPLIT + 2, :, :], -1.0).then_inc(minus_ready, 1)
            pool.wait_ge(minus_ready, 1)
            pool.wait_ge(q1_ready, 1)
            pool.wait_ge(k1_ready, 1)
            stack_group(pool, 1, 0)
            pool.wait_ge(q2_ready, 1)
            stack_group(pool, 1, 2)
            third_part(pool, k_rest, k_part, k_rest_ready, k2_ready, k3_ready)
            third_part(pool, q_rest, q_part, q_rest_ready, q2_ready, q3_ready)
            pool.wait_ge(bv_in, 16)
            pool.wait_ge(v_copied, 1)
            nc.gpsimd.tensor_tensor(v_ones[:, :, :, 0:DH], v_sb[:].rearrange("p t (h d) -> p t h d", h=H),
                                    bv_sb[:].rearrange("p (o h d) -> p o h d", o=1, h=H)
                                            .broadcast_to([P, NT, H, DH]),
                                    ALU.add).then_inc(v_ready, 1)
            def mask_probs(s):
                c, tiles = STEPS[s]
                pool.wait_ge(edge_ready, CHUNKS[c][0] // HALF + 1)
                pool.wait_ge(probs_ready, s + 1)
                p = by_head(probs[:, s, :], c).bitcast(I32)
                on = edge[:, tiles[0]:tiles[-1] + 1, targets(c)].rearrange("p t (o b) -> p t o b", o=1)
                nc.gpsimd.tensor_tensor(p, p, on.broadcast_to(list(p.shape)), ALU.mult).then_inc(pool_masked, 1)

            mask_for_max(nc.gpsimd, 1)
            for s in BY_POOL:
                mask_probs(s)
            pool.wait_ge(x_in, 16)
            pool.wait_ge(bo_in, 16)
            for t in range(BT // P):
                nc.gpsimd.tensor_tensor(xb[:, t, :], x_sb[:, t, :], bo_sb[:], ALU.add).then_inc(xb_ready, 1)

        @block.scalar
        def _(act):
            act.dma_start(kin_sb[:], kin).then_inc(kin_in, 16)
            act.dma_start(bv_sb[:], bv.partition_broadcast(P)).then_inc(bv_in, 16)
            act.wait_ge(zeros_ready, 1)
            nc.scalar.activation(one[:], zeros[:, 0:1], ACT.Exp).then_inc(tables_loaded, 1)
            act.wait_ge(q_proj, 1)
            nc.scalar.activation(q_part[0], ps_q, ACT.Identity, bias=b_q).then_inc(q1_ready, 1)
            act.wait_ge(k_proj, 1)
            nc.scalar.activation(k_part[0], ps_k, ACT.Identity, bias=b_k).then_inc(k1_ready, 1)
            act.wait_ge(v_proj, 1)
            nc.scalar.activation(v_sb[:], ps_v, ACT.Copy).then_inc(v_copied, 1)

            def mask_rows(half):
                act.wait_ge(mask_turned, half + 1)
                bs = slice(HALF * half, HALF * (half + 1))
                nc.scalar.activation(mask_t[:, :, bs], misc_t, ACT.Copy).then_inc(mask_t_ready, 1)

            def edges(half):
                act.wait_ge(mask_t_ready, half + 1)
                bs = slice(HALF * half, HALF * (half + 1))
                nc.scalar.activation(edge[:, :, bs], mask_t[:, :, bs], ACT.Copy, bias=1.0,
                                     scale=1.0 / BIG).then_inc(edge_ready, 1)

            def shift_rows(c):
                quad = CHUNKS[c][2]
                act.wait_ge(shift_turned, c + 1)
                nc.scalar.activation(q_stack[SPLIT:SPLIT + 2, QUAD * quad:QUAD * (quad + 1), targets(c)],
                                     shift_view(c)[SPLIT:SPLIT + 2, :, :], ACT.Copy).then_inc(shift_in_stack, 1)

            def deviation(part):
                act.wait_ge(eps_ready, 1)
                act.wait_ge(aggregated, tiles_of(part).stop)
                nc.scalar.activation(std[:, tiles_of(part), :], mean_var[:, tiles_of(part), 1:2], ACT.Sqrt,
                                     bias=eps[:]).then_inc(std_ready, 1)

            mask_rows(0)
            edges(0)
            shift_rows(0)
            for s in range(LAST + 1):
                shifts = [shift_after(u) for u in units_in(s) if shift_after(u) is not None]
                for n in shifts:
                    if n in SHIFT_FIRST:
                        shift_rows(n)
                if s < len(STEPS):
                    act.wait_ge(step_scored, s + 1)
                    nc.scalar.activation(probs[:, s, :], ps_s[s % 2][:], ACT.Exp, scale=SCALE).then_inc(probs_ready, 1)
                if s - PV_LAG in LAST_STEP and LAST_STEP.index(s - PV_LAG) not in O_BY_DVE:
                    copy_o(act, LAST_STEP.index(s - PV_LAG))
                for n in shifts:
                    if n not in SHIFT_FIRST:
                        shift_rows(n)
                for stage, n in stages_in(s):
                    if stage == "mask":
                        mask_rows(n)
                        if any(STEPS[m][0] >= 3 for m in BY_POOL):
                            edges(n)
                    if stage == "shift":
                        shift_rows(n)
                    if stage == "back" and n not in BACK_BY_DVE:
                        copy_back(act, n)
                    if stage == "root":
                        deviation(n)

        @block.vector
        def _(dve):
            nc.vector.memset(zeros[:], 0.0).then_inc(zeros_ready, 1)
            nc.vector.memset(eps[:], EPS).then_inc(eps_ready, 1)
            nc.vector.memset(guard[:], TINY).then_inc(guard_set, 1)
            dve.wait_ge(guard_set, 1)
            for g in range(QUAD):
                nc.vector.memset(guard[COL * g:COL * g + DH, :], 0.0).then_inc(guard_ready, 1)
            dve.wait_ge(consts_ready, 2)
            nc.vector.tensor_reduce(head_sums[:], ident[:, 0:P // 2].rearrange("p (d g) -> p g d", g=QUAD), AX.X,
                                    ALU.add).then_inc(head_summed, 1)
            dve.wait_ge(head_summed, 1)
            nc.vector.tensor_copy(head_rows[:], head_sums[:]).then_inc(head_rows_ready, 1)
            dve.wait_ge(kin_in, 16)
            nc.vector.tensor_scalar(msg[:], kin_sb[:, 0:BN], e_1, None, ALU.add).then_inc(msg_ready, 1)

            def less_part1(proj, bias, part1, out_, first, done):
                dve.wait_ge(first, 1)
                nc.vector.scalar_tensor_tensor(out=out_, in0=proj, scalar=bias,
                                               in1=part1, op0=ALU.add, op1=ALU.subtract).then_inc(done, 1)

            mask_for_max(nc.vector, 0)
            less_part1(ps_q, b_q, q_part[0], q_part[1], q1_ready, q2_ready)
            single_heads(dve, 0)
            dve.wait_ge(q2_ready, 1)
            single_heads(dve, 1)
            less_part1(ps_k, b_k, k_part[0], k_part[1], k1_ready, k2_ready)
            less_part1(ps_k, b_k, k_part[0], k_rest[:], k1_ready, k_rest_ready)
            less_part1(ps_q, b_q, q_part[0], q_rest[:], q1_ready, q_rest_ready)

            def unit_max(u):
                c, i, g = UNITS[u]
                b = CHUNKS[c][0] // P + i
                dve.wait_ge(mask_max_ready[b // TPH], 1)
                dve.wait_ge(unit_scored, u + 1)
                if u >= 2:
                    dve.wait_ge(unit_maxed, u - 1)
                nc.vector.tensor_tensor_reduce(masked[:, u % 2, :], ps_max[u % 2][:],
                                               mask_max[:, b, :], 1.0, FLOOR,
                                               ALU.add, ALU.max, peak[:, u:u + 1]).then_inc(unit_maxed, 1)
                if u + 1 in FIRST_UNIT:
                    shift_parts(c)

            def mask_probs(s):
                c, tiles = STEPS[s]
                dve.wait_ge(cap_ready, 1)
                dve.wait_ge(probs_ready, s + 1)
                p = by_head(probs[:, s, :], c)
                most = cap[:, tiles[0]:tiles[-1] + 1, targets(c)].rearrange("p t (o b) -> p t o b", o=1)
                nc.vector.tensor_tensor(p, p, most.broadcast_to(list(p.shape)), ALU.min).then_inc(dve_masked, 1)

            def caps(half):
                dve.wait_ge(mask_t_ready, half + 1)
                bs = slice(HALF * half, HALF * (half + 1))
                nc.vector.tensor_scalar(cap[:, :, bs], mask_t[:, :, bs], BIG, None, ALU.add).then_inc(cap_ready, 1)

            def shift_parts(c):
                us = slice(FIRST_UNIT[c], FIRST_UNIT[c + 1])
                dve.wait_ge(unit_maxed, FIRST_UNIT[c + 1])
                nc.vector.tensor_copy(peak1[:, us], peak[:, us]).then_inc(shift_part1, 1)
                nc.vector.scalar_tensor_tensor(out=shift_part[:, us, 0], in0=peak[:, us], scalar=LEAST,
                                               in1=peak[:, us], op0=ALU.is_gt, op1=ALU.mult).then_inc(shift_guarded, 1)
                dve.wait_ge(shift_part1, c + 1)
                nc.vector.tensor_tensor(shift_part[:, us, 1], peak[:, us], peak1[:, us],
                                        ALU.subtract).then_inc(shift_ready, 1)

            def normalise(c):
                b, w, quad = CHUNKS[c]
                us = slice(FIRST_UNIT[c], FIRST_UNIT[c + 1])
                turned = turned_of(c)[:, 0:w].rearrange("p (i g j) -> p i g j", i=w // P, g=QUAD)
                dve.wait_ge(o_turned, c + 1)
                nc.vector.reciprocal(r_denom[:, us], turned[:, :, :, DH:DH + 1]).then_inc(inverted, 1)
                dve.wait_ge(inverted, c + 1)
                out_ = o_norm[:, b // P:(b + w) // P, QUAD * quad:QUAD * (quad + 1), :]
                nc.vector.tensor_tensor(out_, turned[:, :, :, 0:DH],
                                        r_denom[:, us].rearrange("p (i g o) -> p i g o", i=w // P, o=1)
                                                      .broadcast_to(list(out_.shape)), ALU.mult).then_inc(o_ready, 1)

            def residual(part):
                ts = tiles_of(part)
                dve.wait_ge(projected, part + 1)
                dve.wait_ge(xb_ready, BT // P)
                nc.vector.tensor_tensor(res[:, ts, :], out_of(part)[:, 0:PARTS[part][1]].rearrange(
                    "p (t d) -> p t d", d=D), xb[:, ts, :], ALU.add).then_inc(res_ready, 1)

            def moments(part):
                ts = tiles_of(part)
                dve.wait_ge(res_ready, part + 1)
                for t in range(ts.start, ts.stop):
                    nc.vector.bn_stats(stats[:, t, :], res[:, t, :]).then_inc(stats_ready, 1)
                for t in range(ts.start, ts.stop):
                    dve.wait_ge(stats_ready, t + 1)
                    nc.vector.bn_aggr(mean_var[:, t, :], stats[:, t, :]).then_inc(aggregated, 1)

            def finish(part):
                ts = tiles_of(part)
                dve.wait_ge(std_ready, part + 1)
                nc.vector.reciprocal(rstd[:, ts, :], std[:, ts, :]).then_inc(rstd_ready, 1)
                dve.wait_ge(rstd_ready, part + 1)
                for t in range(ts.start, ts.stop):
                    nc.vector.tensor_scalar(y_sb[:, t, :], res[:, t, :], mean_var[:, t, 0:1], rstd[:, t, :],
                                            ALU.subtract, ALU.mult).then_inc(y_ready, 1)

            for u in range(AHEAD):
                unit_max(u)
            for s in range(LAST + 1):
                for u in units_in(s):
                    unit_max(u)
                if s - 1 in BY_DVE:
                    mask_probs(s - 1)
                if s - PV_LAG in LAST_STEP and LAST_STEP.index(s - PV_LAG) in O_BY_DVE:
                    copy_o(dve, LAST_STEP.index(s - PV_LAG))
                for stage, n in stages_in(s):
                    if stage == "cap":
                        caps(n)
                    if stage == "turn":
                        normalise(n)
                    if stage == "back" and n in BACK_BY_DVE:
                        copy_back(dve, n)
                    if stage == "out":
                        residual(n)
                    if stage == "stats":
                        moments(n)
                    if stage == "finish":
                        finish(n)

        @block.tensor
        def _(pe):
            def keep_warm(n):
                for _ in range(n):
                    nc.tensor.matmul(ps_o[:], zeros[:, 0:P], zeros[:], start=True, stop=True)

            pe.wait_ge(zeros_ready, 1)
            keep_warm(WARM)
            pe.wait_ge(qin_in, 16)
            nc.tensor.matmul(ps_q, w_q, qin_sb[:, 0:BT], start=True, stop=True).then_inc(q_proj, 1)
            pe.wait_ge(msg_ready, 1)
            nc.tensor.matmul(ps_k, w_k, msg[:], start=True, stop=True).then_inc(k_proj, 1)
            pe.wait_ge(vin_in, 16)
            v_out = ps_v.rearrange("p (t d) -> p t d", t=NT)
            for t in range(NT):
                last = nc.tensor.matmul(v_out[:, t, :], msg[:, t * P:(t + 1) * P], w_v, start=True, stop=True)
            last.then_inc(v_proj, 1)

            def turn_mask(half):
                pe.wait_ge(mask_max_ready[half], 1)
                misc_free(pe, "mask", half)
                for i in range(TPH):
                    for t in range(NT):
                        last = nc.tensor.transpose(misc_t[:, t, P * i:P * (i + 1)],
                                                   mask_max[:, TPH * half + i, P * t:P * (t + 1)], ident[:])
                last.then_inc(mask_turned, 1)

            def unit_scores(u):
                c, i, g = UNITS[u]
                b0, _, quad = CHUNKS[c]
                h, b = QUAD * quad + g, b0 + P * i
                rows = MAXROWS if c == 1 else SPLIT
                if u == FIRST_UNIT[2]:
                    for group in stacked[1]:
                        pe.wait_ge(group, 16)
                if u >= 2:
                    pe.wait_ge(unit_maxed, u - 1)
                if c == 0:
                    for q, k in ((0, 0), (0, 1), (1, 0)):
                        last = nc.tensor.matmul(ps_max[u % 2][:], q_heads[:, q, g, :], k_part[k],
                                                start=(q, k) == (0, 0), stop=q == 1)
                    last.then_inc(unit_scored, 1)
                    return
                nc.tensor.matmul(ps_max[u % 2][:], q_stack[0:rows, h, b:b + P], k_stack[0:rows, h, :],
                                 start=True, stop=True).then_inc(unit_scored, 1)
                if shift_after(u) is not None:
                    turn_shift(shift_after(u))

            def turn_shift(c):
                pe.wait_ge(shift_guarded, c + 1)
                pe.wait_ge(shift_ready, c + 1)
                misc_free(pe, "shift", c)
                for u in range(FIRST_UNIT[c], FIRST_UNIT[c + 1]):
                    _, i, g = UNITS[u]
                    last = nc.tensor.transpose(shift_view(c)[SPLIT:SPLIT + 2, g, P * i:P * (i + 1)],
                                               shift_part[:, u, :], ident[:])
                last.then_inc(shift_turned, 1)

            def step_scores(s, bank):
                c, tiles = STEPS[s]
                b, w, quad = CHUNKS[c]
                pe.wait_ge(shift_in_stack, c + 1)
                if s >= 2:
                    pe.wait_ge(probs_ready, s - 1)
                pe.wait_ge(mask_t_ready, b // HALF + 1)
                scores = ps_s[s % 2]
                t = tiles[bank % len(tiles)]
                heads = range(2 * bank, 2 * bank + 2) if w == HALF else range(QUAD)
                if s not in BY_POOL + BY_DVE:
                    mask = mask_t[:, t, targets(c)].rearrange("p (o b) -> p o b", o=1)
                    nc.tensor.matmul(scores[:, bank, :], ident[:], mask.broadcast_to([P, len(heads), w]),
                                     start=True, stop=False, skip_group_check=True)
                for n, g in enumerate(heads):
                    h = QUAD * quad + g
                    last = nc.tensor.matmul(scores[:, bank, w * n:w * (n + 1)], k_stack[0:ROWS, h, t * P:(t + 1) * P],
                                            q_stack[0:ROWS, h, targets(c)], start=s in BY_POOL + BY_DVE, stop=True,
                                            skip_group_check=True)
                if bank == 1:
                    last.then_inc(step_scored, 1)

            def step_values(s):
                c, tiles = STEPS[s]
                _, w, quad = CHUNKS[c]
                if c >= 1 and STEPS[s - 1][0] != c:
                    if c in (1, 2, 4):
                        pe.wait_ge(o_copied[c - 1 if c < 4 else 2], 1)
                    if c == 3:
                        pe.wait_ge(unit_maxed, len(UNITS))
                    if c == 5:
                        pe.wait_ge(probs_ready, len(STEPS) - 1)
                if s in BY_POOL:
                    pe.wait_ge(pool_masked, BY_POOL.index(s) + 1)
                elif s in BY_DVE:
                    pe.wait_ge(dve_masked, BY_DVE.index(s) + 1)
                else:
                    pe.wait_ge(probs_ready, s + 1)
                p = by_head(probs[:, s, :], c)
                for n, t in enumerate(tiles):
                    for g in range(QUAD):
                        last = nc.tensor.matmul(sums_of(c)[COL * g:COL * (g + 1), 0:w],
                                                v_ones[:, t, QUAD * quad + g, :],
                                                p[:, n, g, :], start=(t == 0), stop=(t == NT - 1))
                if t == NT - 1:
                    last.then_inc(chunk_summed, 1)

            def turn_o(c):
                if c < len(CHUNKS) - 1:
                    misc_free(pe, "turn", c)
                else:
                    pe.wait_ge(probs_ready, len(STEPS))
                pe.wait_ge(o_copied[c], 1)
                for i in range(CHUNKS[c][1] // P):
                    last = nc.tensor.transpose(turned_of(c)[:, P * i:P * (i + 1)],
                                               o_sb[:, c, P * i:P * (i + 1)], ident32[:])
                last.then_inc(o_turned, 1)

            def turn_back(part):
                pe.wait_ge(o_ready, IN_PART[part])
                pe.wait_ge(unit_maxed, len(UNITS))
                if part == 1:
                    pe.wait_ge(back_ready[0], 1)
                for i, t in enumerate(range(tiles_of(part).start, tiles_of(part).stop)):
                    last = nc.tensor.transpose(back_of(part)[:, P * i:P * (i + 1)],
                                               o_norm[:, t, :, :].rearrange("p h d -> p (h d)"), ident32[:])
                last.then_inc(back_turned, 1)

            def project(part):
                pe.wait_ge(back_ready[part], 1)
                if part == 1:
                    pe.wait_ge(res_ready, part)
                for i, t in enumerate(range(tiles_of(part).start, tiles_of(part).stop)):
                    last = nc.tensor.matmul(out_of(part)[:, D * i:D * (i + 1)], o_back[:, t, :],
                                            vin_sb[:, D:2 * D], start=True, stop=True)
                last.then_inc(projected, 1)

            pe.wait_ge(consts_ready, 2)
            turn_mask(0)
            pe.wait_ge(k2_ready, 1)
            pe.wait_ge(q_heads_ready[0], 1)
            pe.wait_ge(q_heads_ready[1], 1)
            for u in range(FIRST_UNIT[1]):
                unit_scores(u)
            pe.wait_ge(minus_ready, 1)
            for i in range(3):
                pe.wait_ge(stacked[0][i], 16)
            for u in range(FIRST_UNIT[1], AHEAD):
                unit_scores(u)
                keep_warm(WARM_UNIT)
            for i in range(3, len(GROUPS)):
                pe.wait_ge(stacked[0][i], 16)
            pe.wait_ge(v_ready, 1)
            pe.wait_ge(ones_ready, 1)
            for s in range(LAST + 1):
                units = list(units_in(s))
                for what in PE_ORDER[min(s, len(PE_ORDER) - 1)]:
                    if what in "01" and s < len(STEPS):
                        step_scores(s, int(what))
                    if what == "u" and units:
                        unit_scores(units.pop(0))
                    if what == "v" and 0 <= s - PV_LAG < len(STEPS):
                        step_values(s - PV_LAG)
                for u in units:
                    unit_scores(u)
                for stage, n in stages_in(s):
                    if stage == "mask":
                        turn_mask(n)
                    if stage == "shift":
                        turn_shift(n)
                    if stage == "turn":
                        turn_o(n)
                    if stage == "back":
                        turn_back(n)
                    if stage == "out":
                        project(n)


def kernel(x, adj, L0_gnn_h_neigh, L0_gnn_Wq, L0_gnn_bq, L0_gnn_Wk, L0_gnn_bk, L0_gnn_Wv, L0_gnn_bv,
           L0_gnn_Wo, L0_gnn_bo, L0_gnn_E):
    import concourse.bacc as bacc
    from concourse.bass_utils import run_bass_kernel_spmd

    x, adj = np.asarray(x), np.asarray(adj)

    def by_dim(a):
        return a.reshape(*a.shape[:-1], H // QUAD, QUAD, DH).swapaxes(-1, -2).reshape(a.shape)

    arrays = {
        "kin": np.concatenate([np.asarray(L0_gnn_h_neigh).T, by_dim(np.asarray(L0_gnn_Wk).T),
                               by_dim(np.asarray(L0_gnn_bk))[:, None],
                               np.asarray(L0_gnn_E).T], axis=1),
        "qin": np.concatenate([x.T, by_dim(np.asarray(L0_gnn_Wq).T), by_dim(np.asarray(L0_gnn_bq))[:, None]], axis=1),
        "vin": np.concatenate([np.asarray(L0_gnn_Wv).T, np.asarray(L0_gnn_Wo).T], axis=1),
        "x": x,
        "bv": np.asarray(L0_gnn_bv),
        "bo": np.asarray(L0_gnn_bo),
        "adj": adj,
    }
    arrays = {name: np.ascontiguousarray(a) for name, a in arrays.items()}
    nc = bacc.Bacc("TRN2", target_bir_lowering=False, num_devices=1)
    args = [nc.dram_tensor(name, a.shape, mybir.dt.from_np(a.dtype), kind="ExternalInput").ap()
            for name, a in arrays.items()]
    out = nc.dram_tensor("out", (BT, D), F32, kind="ExternalOutput").ap()
    attention_kernel(nc, *args, out)
    result = run_bass_kernel_spmd(nc, [arrays], core_ids=[0])
    return result.results[0]["out"]
```
